# Optimizing a Trainium2 kernel written in Bass

```python
import numpy as np
import jax
import jax.numpy as jnp

def _softmax(x, axis=-1):
    return jax.nn.softmax(x, axis=axis)

def _gelu(x):
    return jax.nn.gelu(x, approximate=True)

def _silu(x):
    return jax.nn.silu(x)

def _sigmoid(x):
    return jax.nn.sigmoid(x)

def _layernorm(x, axis=-1, eps=1e-05):
    m = jnp.mean(x, axis=axis, keepdims=True)
    v = jnp.var(x, axis=axis, keepdims=True)
    return (x - m) / jnp.sqrt(v + eps)

def _scatter_add(tgt, idx, src, axis=0):
    return tgt.at[idx].add(src)

def _segment_sum(src, seg, n):
    return jax.ops.segment_sum(src, seg, n)
kernel_name = 'mk_seq_postln_d1_jaxref_r4_65d54b'

def setup_inputs(seed: int=0):
    np.random.seed(seed)
    _w = jnp.asarray

    def _L0_attn_setup():
        import jax, jax.numpy as jnp
        import numpy as np
        D_MODEL = 256
        N_HEAD = 16
        HEAD_DIM = D_MODEL // N_HEAD
        EPS = 1e-06
        B, T = (4, 256)

        def _eml(x, agg, eps=EPS):
            return jnp.log(jnp.abs(x) + eps) - jnp.log(agg + eps)

        def _split_heads(t):
            b, s, _ = t.shape
            return t.reshape(b, s, N_HEAD, HEAD_DIM).transpose(0, 2, 1, 3)
        key = jax.random.key(seed)
        k0, k1, k2, k3 = jax.random.split(key, 4)
        x = jax.random.normal(k0, (B, T, D_MODEL), dtype=jnp.float32)
        bound = 0.1 / np.sqrt(D_MODEL)
        w_qkv = jax.random.uniform(k1, (3 * D_MODEL, D_MODEL), jnp.float32, -bound, bound)
        w_ky = jax.random.uniform(k2, (D_MODEL, D_MODEL), jnp.float32, -bound, bound)
        w_proj = jax.random.uniform(k3, (D_MODEL, D_MODEL), jnp.float32, -bound, bound)
        return {'x': x, 'w_qkv': w_qkv, 'w_ky': w_ky, 'w_proj': w_proj}
    _L0_attn_in = _L0_attn_setup()

    def _L0_ffn_setup():
        import jax, jax.numpy as jnp
        import numpy as np
        D_IN, D_HID = (256, 1024)

        def _ternary(key, shape):
            return jax.random.randint(key, shape, -1, 2).astype(jnp.float32)

        def _tlin(x, w, s):
            return jnp.einsum('bsi,oi->bso', x, w) * s
        key = jax.random.key(seed)
        ks = jax.random.split(key, 12)
        inv = lambda fan: 1.0 / np.sqrt(fan).astype(np.float32)
        return {'x': jax.random.normal(ks[0], (4, 512, D_IN), dtype=jnp.float32), 'w1_w': _ternary(ks[1], (D_HID, D_IN)), 'w1_s': jax.random.uniform(ks[2], (D_HID,), dtype=jnp.float32) * inv(D_IN), 'w2_w': _ternary(ks[3], (D_HID, D_IN)), 'w2_s': jax.random.uniform(ks[4], (D_HID,), dtype=jnp.float32) * inv(D_IN), 'h1_w': _ternary(ks[5], (D_HID, D_HID)), 'h1_s': jax.random.uniform(ks[6], (D_HID,), dtype=jnp.float32) * inv(D_HID), 'h2_w': _ternary(ks[7], (D_HID, D_HID)), 'h2_s': jax.random.uniform(ks[8], (D_HID,), dtype=jnp.float32) * inv(D_HID), 'w3_w': _ternary(ks[9], (D_IN, D_HID)), 'w3_s': jax.random.uniform(ks[10], (D_IN,), dtype=jnp.float32) * inv(D_HID)}
    _L0_ffn_in = _L0_ffn_setup()
    _d = {'L0_attn_x': _L0_attn_in['x'], 'L0_attn_w_qkv': _L0_attn_in['w_qkv'], 'L0_attn_w_ky': _L0_attn_in['w_ky'], 'L0_attn_w_proj': _L0_attn_in['w_proj'], 'L0_ffn_w1_w': _L0_ffn_in['w1_w'], 'L0_ffn_w1_s': _L0_ffn_in['w1_s'], 'L0_ffn_w2_w': _L0_ffn_in['w2_w'], 'L0_ffn_w2_s': _L0_ffn_in['w2_s'], 'L0_ffn_h1_w': _L0_ffn_in['h1_w'], 'L0_ffn_h1_s': _L0_ffn_in['h1_s'], 'L0_ffn_h2_w': _L0_ffn_in['h2_w'], 'L0_ffn_h2_s': _L0_ffn_in['h2_s'], 'L0_ffn_w3_w': _L0_ffn_in['w3_w'], 'L0_ffn_w3_s': _L0_ffn_in['w3_s']}
    _x0 = _d['L0_attn_x']
    _d['L0_attn_x'] = jax.random.normal(jax.random.fold_in(jax.random.key(seed), 1), (8, 512, 256), dtype=_x0.dtype)
    del _x0
    return _d

def reference(L0_attn_x, L0_attn_w_qkv, L0_attn_w_ky, L0_attn_w_proj, L0_ffn_w1_w, L0_ffn_w1_s, L0_ffn_w2_w, L0_ffn_w2_s, L0_ffn_h1_w, L0_ffn_h1_s, L0_ffn_h2_w, L0_ffn_h2_s, L0_ffn_w3_w, L0_ffn_w3_s):

    def _L0_attn_ref(x, w_qkv, w_ky, w_proj):
        import jax, jax.numpy as jnp
        import numpy as np
        D_MODEL = 256
        N_HEAD = 16
        HEAD_DIM = D_MODEL // N_HEAD
        EPS = 1e-06
        B, T = (4, 256)

        def _eml(x, agg, eps=EPS):
            return jnp.log(jnp.abs(x) + eps) - jnp.log(agg + eps)

        def _split_heads(t):
            b, s, _ = t.shape
            return t.reshape(b, s, N_HEAD, HEAD_DIM).transpose(0, 2, 1, 3)
        b, t, _ = x.shape
        qkv = x @ w_qkv.T
        q, k, v = jnp.split(qkv, 3, axis=-1)
        q, k, v = (_split_heads(q), _split_heads(k), _split_heads(v))
        scale = 1.0 / np.sqrt(HEAD_DIM)
        L = jnp.einsum('bhqd,bhkd->bhqk', q, k) * scale
        mask = jnp.tril(jnp.ones((t, t), dtype=L.dtype))[None, None]
        k_y = _split_heads(x @ w_ky.T)
        L_y = jnp.einsum('bhqd,bhkd->bhqk', q, k_y) * scale
        agg = jnp.sum(jnp.exp(jnp.clip(L_y, -15.0, 15.0)) * mask, axis=-1, keepdims=True) + EPS
        r = _eml(L, agg)
        w = jax.nn.softplus(r) * mask
        A = w / (jnp.sum(w, axis=-1, keepdims=True) + EPS)
        out = jnp.einsum('bhqk,bhkd->bhqd', A, v)
        out = out.transpose(0, 2, 1, 3).reshape(b, t, D_MODEL)
        return out @ w_proj.T

    def _L0_ffn_ref(x, w1_w, w1_s, w2_w, w2_s, h1_w, h1_s, h2_w, h2_s, w3_w, w3_s):
        import jax, jax.numpy as jnp
        import numpy as np
        D_IN, D_HID = (256, 1024)

        def _ternary(key, shape):
            return jax.random.randint(key, shape, -1, 2).astype(jnp.float32)

        def _tlin(x, w, s):
            return jnp.einsum('bsi,oi->bso', x, w) * s
        h = jax.nn.silu(_tlin(x, w1_w, w1_s)) * _tlin(x, w2_w, w2_s)
        h = jax.nn.gelu(_tlin(h, h1_w, h1_s), approximate=False)
        h = jax.nn.gelu(_tlin(h, h2_w, h2_s), approximate=False)
        return _tlin(h, w3_w, w3_s)
    x = L0_attn_x
    x = _layernorm(x + _L0_attn_ref(x, L0_attn_w_qkv, L0_attn_w_ky, L0_attn_w_proj), axis=-1)
    x = _layernorm(x + _L0_ffn_ref(x, L0_ffn_w1_w, L0_ffn_w1_s, L0_ffn_w2_w, L0_ffn_w2_s, L0_ffn_h1_w, L0_ffn_h1_s, L0_ffn_h2_w, L0_ffn_h2_s, L0_ffn_w3_w, L0_ffn_w3_s), axis=-1)
    return x

_drawn_inputs = setup_inputs


def setup_inputs(seed=0):
    import zlib

    import numpy as np

    out = dict(_drawn_inputs(seed))
    spreads = {}
    factors = {'L0_attn_w_qkv': 8.0,
     'L0_attn_w_ky': 8.0,
     'L0_attn_w_proj': 8.0,
     'L0_ffn_w1_w': 8.0,
     'L0_ffn_w1_s': 8.0,
     'L0_ffn_w2_w': 8.0,
     'L0_ffn_w2_s': 8.0,
     'L0_ffn_h1_w': 8.0,
     'L0_ffn_h1_s': 8.0,
     'L0_ffn_h2_w': 8.0,
     'L0_ffn_h2_s': 8.0,
     'L0_ffn_w3_w': 8.0,
     'L0_ffn_w3_s': 8.0}
    for name, (base, spread) in spreads.items():
        noise = np.random.default_rng([zlib.crc32(name.encode()), seed]).standard_normal(out[name].shape)
        drawn = base * np.exp(spread * noise) if base else spread * noise
        out[name] = jnp.asarray(drawn.astype(out[name].dtype))
    for name, factor in factors.items():
        out[name] = (out[name] * factor).astype(out[name].dtype)
    return out
```

```python
import math
from contextlib import ExitStack

import numpy as np

import concourse.bass as bass
from concourse import mybir

F32 = mybir.dt.float32
F32R = mybir.dt.float32r
I32 = mybir.dt.int32
ALU = mybir.AluOpType
ACT = mybir.ActivationFunctionType
AX = mybir.AxisListType

P = 128
BATCH, T, D = 8, 512, 256
H, HD = 16, 16
F = 1024
TI = T // P
DT = D // P
FT = F // P
HU = H // 2
PAIRS = HU // 2
UNITS = 2 * BATCH
COPIES = 4
VW = HD + 1
EPS = 1e-6
LN_EPS = 1e-5
CLIP = 15.0
CHUNKS = 3
W_AT = (0, 512, 1024, 896)
W_COLS = 1280
STACK_DMAS = 2 * COPIES
LN_STEPS = 3 * TI + 5
ATT_STEPS = 6


class Unit:

    def __init__(self, batch, half):
        self.batch, self.half = batch, half
        self.index = 2 * batch + half

    def shift(self, n):
        half = self.half + n
        return Unit(self.batch + half // 2, half % 2)


def reach(engine, sem, value):
    if isinstance(value, int) and value <= 0:
        return
    engine.wait_ge(sem, value)


def reach_alone(engine, sem, value, passed):
    reach(engine, sem, value)
    engine.sem_inc(passed, 1)


def attention_phase(nc, a, x1):
    with ExitStack() as ctx:
        def sb(name, shape, dt=F32):
            return ctx.enter_context(nc.sbuf_tensor(name, shape, dt))

        def sem(name):
            return ctx.enter_context(nc.semaphore(name))

        def bank(name):
            return ctx.enter_context(nc.psum_tensor(name, [P, 512], F32))
        y_bank = [bank("y_bank0"), bank("y_bank1"), bank("y_bank2")]
        w_bank = [bank("w_bank0"), bank("w_bank1"), bank("w_bank2")]
        out_bank = bank("out_bank")
        misc = bank("misc_bank")

        w_raw = sb("w_raw", [P, DT, 4, D])
        w_hi = sb("w_hi", [P, DT, 4, D], F32R)
        w_lo = sb("w_lo", [P, DT, 4, D], F32R)
        wp_hi = sb("wp_hi", [P, DT, D], F32R)
        wp_lo = sb("wp_lo", [P, DT, D], F32R)
        ident = sb("ident", [P, P])
        sel = sb("sel", [64, P], F32R)
        tri = sb("tri", [P, 2, P])
        count = sb("count", [P, TI])
        low = sb("low", [P, T])
        xt_raw = sb("xt_raw", [P, DT, T])
        xt_hi = sb("xt_hi", [P, DT, T], F32R)
        xt_lo = sb("xt_lo", [P, DT, T], F32R)
        x_nat = sb("x_nat", [P, TI, D])
        q_full = [sb(f"q_full{t}", [P, T]) for t in range(2)]
        q_hi, q_lo = sb("q_hi", [P, T], F32R), sb("q_lo", [P, T], F32R)
        ky_hi, ky_lo = sb("ky_hi", [P, T], F32R), sb("ky_lo", [P, T], F32R)
        k_hi, k_lo = sb("k_hi", [P, T], F32R), sb("k_lo", [P, T], F32R)
        qc_full = sb("qc_full", [P, T])
        qc_hi, qc_lo = sb("qc_hi", [P, T], F32R), sb("qc_lo", [P, T], F32R)
        q_stack = [sb(f"q_stack{t}", [P, PAIRS, T], F32R) for t in range(2)]
        ky_stack = [sb(f"ky_stack{t}", [P, PAIRS, T], F32R) for t in range(2)]
        k_stack = [sb(f"k_stack{t}", [P, PAIRS, T], F32R) for t in range(2)]
        qc_stack = [sb(f"qc_stack{t}", [P, PAIRS, T], F32R) for t in range(2)]
        v_aug = [sb(f"v_aug{t}", [P, TI, HU, VW]) for t in range(2)]
        E_BUFS = 4
        e_buf = [sb(f"e_buf{i}", [P, T]) for i in range(E_BUFS)]
        agg = [sb(f"agg{t}", [P, TI, HU]) for t in range(2)]
        agg_eps = sb("agg_eps", [P, TI, 2 * HU])
        c_cols = sb("c_cols", [P, TI, 2 * HU])
        c_rows = sb("c_rows", [64, T], F32R)
        w_buf = [sb(f"w_buf{i}", [P, W_COLS]) for i in range(2)]
        att_raw = sb("att_raw", [P, TI, H, VW])
        base = sb("base", [P, TI, H])
        v_sum = sb("v_sum", [P, TI, H, HD])
        base_v = sb("base_v", [P, TI, H, HD])
        base_sum = sb("base_sum", [P, TI, H])
        att_den = sb("att_den", [P, TI * H])
        att_inv = sb("att_inv", [P, TI * H])
        att = sb("att", [P, TI, D])
        att_hi, att_lo = sb("att_hi", [P, DT, T], F32R), sb("att_lo", [P, DT, T], F32R)
        res = sb("res", [P, TI, D])
        stats, mv = sb("stats", [P, TI, 6]), sb("mv", [P, TI, 2])
        var_eps, log_var = sb("var_eps", [P, TI]), sb("log_var", [P, TI])
        root_est, root_a, root_b, root_c, rstd = (sb(f"root{i}", [P, TI]) for i in range(5))

        low_made = sem("low_made")
        weights_in = sem("weights_in")
        weights_split = sem("weights_split")
        xt_in = sem("xt_in")
        xn_in = sem("xn_in")
        xt_split = sem("xt_split")
        xt_hi_made = sem("xt_hi_made")
        k_ready, v_ready = sem("k_ready"), sem("v_ready")
        q_ready, ky_ready = sem("q_ready"), sem("ky_ready")
        k_hi_made, k_lo_made = sem("k_hi_made"), sem("k_lo_made")
        q_hi_made, q_lo_made = sem("q_hi_made"), sem("q_lo_made")
        ky_hi_made, ky_lo_made = sem("ky_hi_made"), sem("ky_lo_made")
        v_copied = sem("v_copied")
        q_stacked = [sem(f"q_stacked{t}") for t in range(2)]
        ky_stacked = [sem(f"ky_stacked{t}") for t in range(2)]
        k_stacked = [sem(f"k_stacked{t}") for t in range(2)]
        qc_stacked = [sem(f"qc_stacked{t}") for t in range(2)]
        y_scores = sem("y_scores")
        exp_done = sem("exp_done")
        e_masked = sem("e_masked")
        e_summed = sem("e_summed")
        cols_step = sem("cols_step")
        rows_ready = sem("rows_ready")
        rows_hi_made, rows_lo_made = sem("rows_hi_made"), sem("rows_lo_made")
        spread_ready = sem("spread_ready")
        qc_made = sem("qc_made")
        qc_hi_made, qc_lo_made = sem("qc_hi_made"), sem("qc_lo_made")
        base_made = sem("base_made")
        v_sum_ready, v_sum_copied = sem("v_sum_ready"), sem("v_sum_copied")
        w_scores = sem("w_scores")
        args_done = sem("args_done")
        ln_done = sem("ln_done")
        w_masked = sem("w_masked")
        pv_done = sem("pv_done")
        att_copied = sem("att_copied")
        att_step = sem("att_step")
        turned = sem("turned")
        turned_hi, turned_lo = sem("turned_hi"), sem("turned_lo")
        proj_ready = sem("proj_ready")
        res_made = sem("res_made")
        ln_step = sem("ln_step")
        log_made, rs_made = sem("log_made"), sem("rs_made")
        x1_stored = sem("x1_stored")
        pool_passed, sp_passed, dve_passed = sem("pool_passed"), sem("sp_passed"), sem("dve_passed")

        rows = [slice(64 * par, 64 * par + 64) for par in range(2)]
        block = ctx.enter_context(nc.Block())

        def y_tiles(c):
            return (((0, 3),), ((0, 2), (384, 0)), ((0, 1),))[c]

        def w_tiles(c):
            return (((0, 0),), ((0, 1), (384, 3)), ((0, 2),))[c]

        def run(slot, fori):
            slot(Unit(0, 0), weights=False)
            slot(Unit(0, 1), x=1)
            slot(Unit(1, 0))
            with fori(1, BATCH - 1) as j:
                slot(Unit(j, 1), x=j + 1, out=j - 1, first_in_loop=True)
                slot(Unit(j + 1, 0))
            slot(Unit(BATCH - 1, 1), out=BATCH - 2, project=False, first_in_loop=True)
            slot(Unit(BATCH, 0), denominators=False)
            slot(Unit(BATCH, 1), denominators=False, weights=False, out=BATCH - 1)

        @block.sync
        def _(sp):
            sp.dma_start(w_raw[:], a["w4"]).then_inc(weights_in, 16)
            sp.dma_start(ident[:], a["ident"]).then_inc(weights_in, 16)
            sp.dma_start(xt_raw[:], a["xt"][0]).then_inc(xt_in, 16)
            sp.dma_start(res[:, 0:DT, :], a["wp"]).then_inc(weights_in, 16)
            sp.dma_start(w_buf[0][0:64, 0:P], a["sel"]).then_inc(weights_in, 16)
            sp.dma_start(tri[:], a["tri"]).then_inc(weights_in, 16)
            sp.dma_start(count[:], a["count"]).then_inc(weights_in, 16)

            def stack(dst, hi, lo, copies, sem):
                for par in range(2):
                    for r, half in enumerate(copies):
                        src = (hi, lo)[half][64 * par:64 * par + 64, :]
                        to = dst[64 * par + HD * r:64 * par + HD * r + HD, :, :]
                        sp.dma_start(to.bitcast(F32), src.bitcast(F32)).then_inc(sem, 16)
            LEFT, RIGHT = (0, 0, 1, 1), (0, 1, 0, 1)
            done = 16 * STACK_DMAS

            def stack_q(u):
                reach(sp, q_hi_made, u.index + 1)
                reach_alone(sp, q_lo_made, u.index + 1, sp_passed)
                reach(sp, y_scores, 24 * (u.index - 1))
                stack(q_stack[u.half], q_hi, q_lo, LEFT, q_stacked[u.half])
                reach(sp, ky_hi_made, u.index + 1)
                reach(sp, ky_lo_made, u.index + 1)
                stack(ky_stack[u.half], ky_hi, ky_lo, RIGHT, ky_stacked[u.half])

            def slot(k, weights=True, denominators=True, project=True, x=None, out=None, first_in_loop=False):
                v = k.shift(-1)
                if x is not None:
                    reach_alone(sp, xt_split, x, sp_passed)
                    sp.dma_start(xt_raw[:], a["xt"][x]).then_inc(xt_in, 16)
                if out is not None:
                    reach_alone(sp, res_made, 2 * out, sp_passed)
                    sp.dma_start(x_nat[:], a["xn"][out]).then_inc(xn_in, 16)
                if weights:
                    reach(sp, qc_hi_made, v.index + 1)
                    reach_alone(sp, qc_lo_made, v.index + 1, sp_passed)
                    reach(sp, w_scores, 24 * (v.index - 1))
                    stack(qc_stack[v.half], qc_hi, qc_lo, RIGHT, qc_stacked[v.half])
                if denominators:
                    reach(sp, k_hi_made, k.index + 1)
                    reach_alone(sp, k_lo_made, k.index + 1, sp_passed)
                    reach(sp, w_scores, 24 * (k.index - 1))
                    stack(k_stack[k.half], k_hi, k_lo, LEFT, k_stacked[k.half])
                    if project:
                        stack_q(k.shift(1))
                if out is not None:
                    reach_alone(sp, ln_step, LN_STEPS * (out + 1), sp_passed)
                    sp.dma_start(x1[out], res[:]).then_inc(x1_stored, 16)

            stack_q(Unit(0, 0))
            run(slot, sp.Fori)
            sp.wait_ge(x1_stored, 16 * BATCH)

        @block.gpsimd
        def _(pool):
            nc.gpsimd.memset(low[:], math.exp(-CLIP)).then_inc(low_made, 1)
            pool.wait_ge(low_made, 1)
            nc.gpsimd.affine_select(out=low[:, T - P:T], in_=low[:, T - P:T], compare_op=ALU.is_ge, fill=0.0, base=0,
                                    pattern=[[-1, P]], channel_multiplier=1).then_inc(low_made, 1)

            def mask_e(k, n):
                for c, (at, blocks) in enumerate(((384, 1), (256, 2), (128, 1))):
                    g = 24 * k.index + 3 * n + c
                    e = e_buf[(3 * n + c) % E_BUFS][:, at:at + P * blocks].rearrange("p (b c) -> p b c", b=blocks)
                    reach_alone(pool, exp_done, g + 1, pool_passed)
                    nc.gpsimd.affine_select(out=e, in_=e, compare_op=ALU.is_ge, fill=0.0, base=0,
                                            pattern=[[0, blocks], [-1, P]], channel_multiplier=1).then_inc(e_masked, 1)

            def mask_w(v, n):
                reach_alone(pool, ln_done, 8 * v.index + n + 1, pool_passed)
                w = w_buf[n % 2]
                for blocks in (w[:, 0:1024].rearrange("p (b c) -> p b c", b=2)[:, :, 0:P],
                               w[:, 896:1152].rearrange("p (b c) -> p b c", b=2)):
                    nc.gpsimd.affine_select(out=blocks, in_=blocks, compare_op=ALU.is_ge, fill=0.0, base=0,
                                            pattern=[[0, 2], [1, P]], channel_multiplier=-1).then_inc(w_masked, 1)

            def slot(k, weights=True, denominators=True, **_):
                if denominators:
                    for n in range(HU):
                        mask_e(k, n)
                if weights:
                    for n in range(HU):
                        mask_w(k.shift(-1), n)
            run(slot, pool.Fori)

        @block.scalar
        def _(act):
            nc.scalar.preload_act_table_set("natural_log_exp_and_others")
            act.wait_ge(weights_in, 96)
            nc.scalar.copy(w_hi[:], w_raw[:]).then_inc(weights_split, 1)
            nc.scalar.copy(wp_hi[:], res[:, 0:DT, :]).then_inc(weights_split, 1)
            nc.scalar.copy(sel[:], w_buf[0][0:64, 0:P]).then_inc(weights_split, 1)

            def split_x(b):
                reach(act, xt_in, 16 * (b + 1))
                reach(act, v_ready, 2 * b)
                nc.scalar.copy(xt_hi[:], xt_raw[:]).then_inc(xt_hi_made, 1)

            def q_split(u):
                reach(act, q_ready, u.index + 1)
                reach(act, qc_made, u.index - 1)
                nc.scalar.mul(q_full[u.half][:], misc[:], HD ** -0.5)
                before = u.shift(-1)
                reach(act, q_stacked[before.half], 16 * STACK_DMAS * (before.batch + 1))
                nc.scalar.mul(q_hi[:], misc[:], HD ** -0.5).then_inc(q_hi_made, 1)

            def ky_split(u):
                reach(act, ky_ready, u.index + 1)
                before = u.shift(-1)
                reach(act, ky_stacked[before.half], 16 * STACK_DMAS * (before.batch + 1))
                nc.scalar.copy(ky_hi[:], misc[:]).then_inc(ky_hi_made, 1)

            def k_split(u):
                reach(act, k_ready, u.index + 1)
                before = u.shift(-1)
                reach(act, k_stacked[before.half], 16 * STACK_DMAS * (before.batch + 1))
                nc.scalar.copy(k_hi[:], misc[:]).then_inc(k_hi_made, 1)

            def v_copy(u):
                reach(act, v_ready, u.index + 1)
                reach(act, pv_done, 8 * (u.index - 1))
                nc.scalar.copy(v_aug[u.half][:, :, :, 0:HD],
                               misc[:].rearrange("p (i h d) -> p i h d", i=TI, h=HU)).then_inc(v_copied, 1)

            def exps(k, n):
                for c in range(CHUNKS):
                    g, cols = 24 * k.index + 3 * n + c, (512, 512, 256)[c]
                    reach(act, y_scores, g + 1)
                    reach(act, e_summed, g + 1 - E_BUFS)
                    nc.scalar.activation(e_buf[(3 * n + c) % E_BUFS][:, 0:cols], y_bank[(3 * n + c) % 3][:, 0:cols],
                                         ACT.Exp).then_inc(exp_done, 1)

            def rows_hi(v):
                reach(act, rows_ready, v.index + 1)
                nc.scalar.copy(c_rows[0:HU, :], misc[0:HU, :]).then_inc(rows_hi_made, 1)

            def qc_split(v):
                reach(act, qc_made, v.index + 1)
                before = v.shift(-1)
                reach(act, qc_stacked[before.half], 16 * STACK_DMAS * (before.batch + 1))
                nc.scalar.copy(qc_hi[:], qc_full[:]).then_inc(qc_hi_made, 1)

            def turn_hi(b, ct):
                reach(act, turned, 2 * b + ct + 1)
                nc.scalar.copy(att_hi[:, ct, :], misc[:]).then_inc(turned_hi, 1)

            def root(b):
                reach(act, ln_step, LN_STEPS * b + 2 * TI + 1)
                nc.scalar.activation(log_var[:], var_eps[:], ACT.Ln).then_inc(log_made, 1)
                reach(act, log_made, b + 1)
                nc.scalar.activation(root_est[:], log_var[:], ACT.Exp, scale=-0.5).then_inc(rs_made, 1)

            def base_make(v):
                reach(act, cols_step, 3 * v.index + 3)
                if v.half == 0:
                    reach(act, att_step, ATT_STEPS * v.batch)
                nc.scalar.activation(base[:, :, HU * v.half:HU * v.half + HU], c_cols[:, :, HU:2 * HU], ACT.Ln,
                                     bias=1.0, scale=EPS).then_inc(base_made, 1)

            def v_sum_copy(v):
                reach(act, v_sum_ready, v.index + 1)
                nc.scalar.copy(v_sum[:, :, HU * v.half:HU * v.half + HU, :],
                               misc[:].rearrange("p (i h d) -> p i h d", i=TI, h=HU)).then_inc(v_sum_copied, 1)

            def logs(v, n):
                reach(act, args_done, 24 * v.index + 3 * n + 3)
                nc.scalar.activation(w_buf[n % 2][:], w_buf[n % 2][:], ACT.Ln, bias=1.0).then_inc(ln_done, 1)

            def out_copy(v, p):
                reach(act, pv_done, 8 * v.index + 2 * p + 2)
                if v.half == 0 and p == 0:
                    reach(act, att_step, ATT_STEPS * v.batch)
                nc.scalar.copy(att_raw[:, :, HU * v.half + 2 * p:HU * v.half + 2 * p + 2, :],
                               out_bank[:, 0:TI * 2 * VW].rearrange("p (i h c) -> p i h c", i=TI, h=2)).then_inc(att_copied, 1)

            def slot(k, weights=True, denominators=True, project=True, x=None, out=None, first_in_loop=False):
                v = k.shift(-1)
                for n in range(HU):
                    if n == 5 and x is not None:
                        split_x(x)
                    if denominators:
                        exps(k, n)
                    if n == 0 and weights:
                        rows_hi(v)
                        base_make(v)
                    if n == 2 and weights:
                        qc_split(v)
                        v_sum_copy(v)
                    if n in (2, 3) and out is not None:
                        turn_hi(out, n - 2)
                    if n == 3 and denominators:
                        k_split(k)
                    if n == 4 and denominators:
                        v_copy(k)
                    if n == 5 and denominators and project:
                        q_split(k.shift(1))
                    if n == 6 and denominators and project:
                        ky_split(k.shift(1))
                    if n == 7 and out is not None:
                        root(out)
                if weights:
                    for n in range(HU):
                        logs(v, n)
                        if n % 2 == 0 and n > 0:
                            out_copy(v, n // 2 - 1)
                    out_copy(v, PAIRS - 1)

            split_x(0)
            q_split(Unit(0, 0))
            ky_split(Unit(0, 0))
            run(slot, act.Fori)

        @block.vector
        def _(dve):
            for t in range(2):
                nc.vector.memset(v_aug[t][:, :, :, HD:VW], 1.0)
            nc.vector.memset(c_rows[:].bitcast(I32), 0)
            dve.wait_ge(weights_in, 96)
            dve.wait_ge(weights_split, 3)
            nc.vector.tensor_tensor(w_lo[:], w_raw[:], w_hi[:].bitcast(F32), ALU.subtract).then_inc(weights_split, 1)
            nc.vector.tensor_tensor(wp_lo[:], res[:, 0:DT, :], wp_hi[:].bitcast(F32), ALU.subtract).then_inc(weights_split, 1)
            dve.wait_ge(low_made, 2)

            def split_x(b):
                reach(dve, xt_hi_made, b + 1)
                nc.vector.tensor_tensor(xt_lo[:], xt_raw[:], xt_hi[:].bitcast(F32), ALU.subtract).then_inc(xt_split, 1)

            def lo_of(lo, hi, made, count, then, scale=1.0):
                reach(dve, made, count)
                nc.vector.scalar_tensor_tensor(out=lo, in0=misc[:], scalar=scale, in1=hi.bitcast(F32),
                                               op0=ALU.mult, op1=ALU.subtract).then_inc(then, 1)

            def stack_free(stacked, u):
                before = u.shift(-1)
                reach(dve, stacked[before.half], 16 * STACK_DMAS * (before.batch + 1))

            def q_split(u):
                stack_free(q_stacked, u)
                lo_of(q_lo[:], q_hi[:], q_hi_made, u.index + 1, q_lo_made, HD ** -0.5)

            def ky_split(u):
                stack_free(ky_stacked, u)
                lo_of(ky_lo[:], ky_hi[:], ky_hi_made, u.index + 1, ky_lo_made)

            def k_split(u):
                stack_free(k_stacked, u)
                lo_of(k_lo[:], k_hi[:], k_hi_made, u.index + 1, k_lo_made)

            def sums(k, n):
                for c in range(CHUNKS):
                    g = 24 * k.index + 3 * n + c
                    reach(dve, e_masked, g + 1)
                    for at, i in y_tiles(c):
                        e = e_buf[(3 * n + c) % E_BUFS][:, at:at + P * (i + 1)]
                        last = nc.vector.scalar_tensor_tensor(out=e, in0=e, scalar=math.exp(CLIP),
                                                              in1=low[:, P * (TI - 1 - i):T], op0=ALU.min, op1=ALU.max,
                                                              accum_out=agg[k.half][:, i, n:n + 1])
                    last.then_inc(e_summed, 1)

            def cols(v):
                reach(dve, e_summed, 24 * (v.index + 1))
                reach(dve, rows_ready, v.index)
                reach(dve, base_made, v.index)
                nc.vector.tensor_scalar(agg_eps[:, :, HU:2 * HU], agg[v.half][:], EPS, EPS, ALU.add, ALU.add).then_inc(cols_step, 1)
                reach(dve, cols_step, 3 * v.index + 1)
                nc.vector.tensor_scalar(agg_eps[:, :, 0:HU], agg_eps[:, :, HU:2 * HU], EPS, None, ALU.add).then_inc(cols_step, 1)
                reach(dve, cols_step, 3 * v.index + 2)
                nc.vector.reciprocal(c_cols[:], agg_eps[:]).then_inc(cols_step, 1)

            def rows_lo(v):
                reach(dve, rows_hi_made, v.index + 1)
                nc.vector.tensor_tensor(c_rows[32:32 + HU, :], misc[0:HU, :], c_rows[0:HU, :].bitcast(F32),
                                        ALU.subtract).then_inc(rows_lo_made, 1)

            def qc_make(v):
                reach(dve, spread_ready, v.index + 1)
                reach(dve, qc_hi_made, v.index)
                reach(dve, qc_lo_made, v.index)
                nc.vector.tensor_tensor(qc_full[:], misc[:], q_full[v.half][:], ALU.mult).then_inc(qc_made, 1)

            def qc_split(v):
                stack_free(qc_stacked, v)
                reach(dve, qc_hi_made, v.index + 1)
                nc.vector.tensor_tensor(qc_lo[:], qc_full[:], qc_hi[:].bitcast(F32), ALU.subtract).then_inc(qc_lo_made, 1)

            def args(v, n):
                reach(dve, pv_done, 8 * v.index + n - 1)
                for c in range(CHUNKS):
                    reach(dve, w_scores, 24 * v.index + 3 * n + c + 1)
                    cols = (512, 512, 256)[c]
                    at = (0, 512, 1024)[c]
                    nc.vector.tensor_scalar(w_buf[n % 2][:, at:at + cols].bitcast(I32), w_bank[c][:, 0:cols].bitcast(I32),
                                            0x7FFFFFFF, None, ALU.bitwise_and).then_inc(args_done, 1)

            def divide(b):
                reach(dve, att_copied, 8 * (b + 1))
                reach(dve, base_made, 2 * (b + 1))
                reach(dve, v_sum_copied, 2 * (b + 1))
                reach(dve, turned, 2 * b)
                raw = att_raw[:].rearrange("p i h c -> p (i h) c")
                start = ATT_STEPS * b
                nc.vector.tensor_tensor(base_v[:].rearrange("p i h d -> p (i h) d"), v_sum[:].rearrange("p i h d -> p (i h) d"),
                                        base[:].rearrange("p i h -> p (i h)").unsqueeze(2).to_broadcast([P, TI * H, HD]),
                                        ALU.mult).then_inc(att_step, 1)
                nc.vector.tensor_tensor(base_sum[:], base[:], count[:].unsqueeze(2).to_broadcast([P, TI, H]),
                                        ALU.mult).then_inc(att_step, 1)
                reach(dve, att_step, start + 2)
                nc.vector.scalar_tensor_tensor(out=att_den[:], in0=raw[:, :, HD], scalar=EPS,
                                               in1=base_sum[:].rearrange("p i h -> p (i h)"),
                                               op0=ALU.add, op1=ALU.add).then_inc(att_step, 1)
                nc.vector.tensor_tensor(base_v[:].rearrange("p i h d -> p (i h) d"), base_v[:].rearrange("p i h d -> p (i h) d"),
                                        raw[:, :, 0:HD], ALU.add).then_inc(att_step, 1)
                reach(dve, att_step, start + 4)
                nc.vector.reciprocal(att_inv[:], att_den[:]).then_inc(att_step, 1)
                reach(dve, att_step, start + 5)
                nc.vector.tensor_tensor(att[:].rearrange("p i (h d) -> p (i h) d", h=H),
                                        base_v[:].rearrange("p i h d -> p (i h) d"),
                                        att_inv[:].unsqueeze(2).to_broadcast([P, TI * H, HD]), ALU.mult).then_inc(att_step, 1)

            def residual(b, half):
                reach(dve, xn_in, 16 * (b + 1))
                reach(dve, x1_stored, 16 * b)
                reach(dve, proj_ready, 2 * b + half + 1)
                two = slice(2 * half, 2 * half + 2)
                nc.vector.tensor_tensor(res[:, two, :], misc[:].rearrange("p (i d) -> p i d", i=2), x_nat[:, two, :],
                                        ALU.add).then_inc(res_made, 1)

            norm = dict(passed=dve_passed, ln_step=ln_step, rs_made=rs_made, res=res, stats=stats, mv=mv, var_eps=var_eps,
                        root_est=root_est, root_a=root_a, root_b=root_b, root_c=root_c, rstd=rstd)

            def slot(k, weights=True, denominators=True, project=True, x=None, out=None, first_in_loop=False):
                v = k.shift(-1)
                if weights:
                    cols(v)
                if out is not None:
                    divide(out)
                for n in range(HU):
                    if n == 5 and x is not None:
                        split_x(x)
                    if denominators:
                        sums(k, n)
                    if n == 0 and weights:
                        rows_lo(v)
                    if n == 1 and weights:
                        qc_make(v)
                    if n == 2 and weights:
                        qc_split(v)
                    if n in (2, 3) and out is not None:
                        lo_of(att_lo[:, n - 2, :], att_hi[:, n - 2, :], turned_hi, 2 * out + n - 1, turned_lo)
                    if n == 3 and denominators:
                        k_split(k)
                    if n in (4, 5) and out is not None:
                        residual(out, n - 4)
                    if n == 5 and denominators and project:
                        q_split(k.shift(1))
                    if n == 6 and out is not None:
                        reach(dve, res_made, 2 * out + 2)
                        norm_statistics(nc, dve, out, norm)
                    if n == 6 and denominators and project:
                        ky_split(k.shift(1))
                    if n == 7 and out is not None:
                        norm_apply(nc, dve, out, norm)
                if weights:
                    for n in range(HU):
                        args(v, n)

            split_x(0)
            q_split(Unit(0, 0))
            ky_split(Unit(0, 0))
            run(slot, dve.Fori)

        @block.tensor
        def _(pe):
            misc_readers = []

            def take_misc(*readers):
                for s, count in misc_readers:
                    reach(pe, s, count)
                misc_readers[:] = readers

            def three(out, left, right, first, last):
                (lh, ll), (rh, rl) = left, right
                nc.tensor.matmul(out, lh, rh, start=first, stop=False)
                nc.tensor.matmul(out, ll, rh, start=False, stop=False)
                return nc.tensor.matmul(out, lh, rl, start=False, stop=last)

            def project_t(u, kind, done):
                reach(pe, xt_split, u.batch + 1)
                m = slice(P * u.half, P * u.half + P)
                for kt in range(DT):
                    mm = three(misc[:], (w_hi[:, kt, kind, m], w_lo[:, kt, kind, m]),
                               (xt_hi[:, kt, :], xt_lo[:, kt, :]), kt == 0, kt == DT - 1)
                mm.then_inc(done, 1)

            def q_proj(u):
                take_misc((q_lo_made, u.index + 1))
                project_t(u, 0, q_ready)

            def ky_proj(u):
                take_misc((ky_lo_made, u.index + 1))
                project_t(u, 1, ky_ready)

            def k_proj(u):
                take_misc((k_lo_made, u.index + 1))
                project_t(u, 2, k_ready)

            def v_proj(u):
                take_misc((v_copied, u.index + 1))
                m = slice(P * u.half, P * u.half + P)
                for i in range(TI):
                    tok = slice(P * i, P * i + P)
                    for kt in range(DT):
                        mm = three(misc[:, tok], (xt_hi[:, kt, tok], xt_lo[:, kt, tok]),
                                   (w_hi[:, kt, 3, m], w_lo[:, kt, 3, m]), kt == 0, kt == DT - 1)
                mm.then_inc(v_ready, 1)

            def scores_y(k, n):
                if n == 0:
                    reach(pe, q_stacked[k.half], 16 * STACK_DMAS * (k.batch + 1))
                    reach(pe, ky_stacked[k.half], 16 * STACK_DMAS * (k.batch + 1))
                r, p = rows[n % 2], n // 2
                q, ky = q_stack[k.half], ky_stack[k.half]
                for c in range(CHUNKS):
                    reach(pe, exp_done, 24 * k.index + 3 * (n - 1) + c + 1)
                    for at, i in y_tiles(c):
                        mm = nc.tensor.matmul(y_bank[c][:, at:at + P * (i + 1)], q[r, p, P * i:P * i + P],
                                              ky[r, p, 0:P * (i + 1)], start=True, stop=True)
                    mm.then_inc(y_scores, 1)

            def scores_w(v, n):
                if n == 0:
                    reach(pe, k_stacked[v.half], 16 * STACK_DMAS * (v.batch + 1))
                    reach(pe, qc_stacked[v.half], 16 * STACK_DMAS * (v.batch + 1))
                r, p = rows[n % 2], n // 2
                k, qc = k_stack[v.half], qc_stack[v.half]
                for c in range(CHUNKS):
                    reach(pe, args_done, 24 * v.index + 3 * (n - 1) + c + 1)
                    for at, j in w_tiles(c):
                        mm = nc.tensor.matmul(w_bank[c][:, at:at + T - P * j], k[r, p, P * j:P * j + P],
                                              qc[r, p, P * j:T], start=True, stop=True)
                    mm.then_inc(w_scores, 1)

            def rows_of_c(v):
                take_misc((rows_lo_made, v.index + 1))
                reach(pe, cols_step, 3 * (v.index + 1))
                for i in range(TI):
                    mm = nc.tensor.transpose(misc[0:HU, P * i:P * i + P], c_cols[:, i, 0:HU], ident[:])
                mm.then_inc(rows_ready, 1)

            def spread_c(v):
                take_misc((qc_made, v.index + 1))
                reach(pe, rows_lo_made, v.index + 1)
                nc.tensor.matmul(misc[:], sel[:], c_rows[:], start=True, stop=True).then_inc(spread_ready, 1)

            def sum_values(v):
                take_misc((v_sum_copied, v.index + 1))
                reach(pe, v_copied, v.index + 1)
                for i in range(TI):
                    for j in range(i + 1):
                        mm = nc.tensor.matmul(misc[:, P * i:P * i + P], tri[:, int(j < i), :],
                                              v_aug[v.half][:, j, :, 0:HD], start=(j == 0), stop=(j == i))
                mm.then_inc(v_sum_ready, 1)

            def weigh(v, n):
                reach(pe, w_masked, 2 * (8 * v.index + n + 1))
                if n == 0:
                    reach(pe, v_copied, v.index + 1)
                if n % 2 == 0:
                    reach(pe, att_copied, 4 * v.index + n // 2)
                for i in range(TI):
                    at = (2 * i + n % 2) * VW
                    for j in range(i + 1):
                        w_at = W_AT[j] + P * (i - j)
                        mm = nc.tensor.matmul(out_bank[:, at:at + VW], w_buf[n % 2][:, w_at:w_at + P],
                                              v_aug[v.half][:, j, n, :], start=(j == 0), stop=(j == i))
                mm.then_inc(pv_done, 1)

            def turn(b, ct):
                take_misc((turned_lo, 2 * b + ct + 1))
                reach(pe, att_step, ATT_STEPS * (b + 1))
                for i in range(TI):
                    mm = nc.tensor.transpose(misc[:, P * i:P * i + P], att[:, i, P * ct:P * ct + P], ident[:])
                mm.then_inc(turned, 1)

            def project_out(b, half):
                take_misc((res_made, 2 * b + half + 1))
                reach(pe, turned_lo, 2 * (b + 1))
                for i2 in range(2):
                    i = 2 * half + i2
                    tok = slice(P * i, P * i + P)
                    for ct in range(DT):
                        mm = three(misc[:, D * i2:D * i2 + D], (att_hi[:, ct, tok], att_lo[:, ct, tok]),
                                   (wp_hi[:, ct, :], wp_lo[:, ct, :]), ct == 0, ct == DT - 1)
                mm.then_inc(proj_ready, 1)

            def slot(k, weights=True, denominators=True, project=True, x=None, out=None, first_in_loop=False):
                v = k.shift(-1)
                if first_in_loop:
                    misc_readers[:] = [(ky_lo_made, k.index + 1)]
                for n in range(HU):
                    if denominators:
                        scores_y(k, n)
                    if n == 0 and weights:
                        rows_of_c(v)
                    if n == 1 and weights:
                        spread_c(v)
                        sum_values(v)
                    if n in (2, 3) and out is not None:
                        turn(out, n - 2)
                    if n == 3 and denominators:
                        k_proj(k)
                    if n == 4 and denominators:
                        v_proj(k)
                    if n in (4, 5) and out is not None:
                        project_out(out, n - 4)
                    if n == 5 and denominators and project:
                        q_proj(k.shift(1))
                    if n == 6 and denominators and project:
                        ky_proj(k.shift(1))
                if weights:
                    for n in range(HU):
                        scores_w(v, n)
                        if n > 0:
                            weigh(v, n - 1)
                    weigh(v, HU - 1)

            pe.wait_ge(weights_split, 5)
            q_proj(Unit(0, 0))
            ky_proj(Unit(0, 0))
            run(slot, pe.Fori)


def norm_statistics(nc, dve, b, s):
    base = LN_STEPS * b
    for i in range(TI):
        nc.vector.bn_stats(s["stats"][:, i, :], s["res"][:, i, :]).then_inc(s["ln_step"], 1)
    reach_alone(dve, s["ln_step"], base + TI, s["passed"])
    for i in range(TI):
        nc.vector.bn_aggr(s["mv"][:, i, :], s["stats"][:, i, :]).then_inc(s["ln_step"], 1)
    reach(dve, s["ln_step"], base + 2 * TI)
    nc.vector.tensor_scalar(s["var_eps"][:], s["mv"][:, :, 1], LN_EPS, None, ALU.add).then_inc(s["ln_step"], 1)


def norm_apply(nc, dve, b, s):
    at = LN_STEPS * b + 2 * TI + 1
    step = s["ln_step"]
    reach(dve, s["rs_made"], b + 1)
    nc.vector.tensor_tensor(s["root_a"][:], s["root_est"][:], s["root_est"][:], ALU.mult).then_inc(step, 1)
    reach(dve, step, at + 1)
    nc.vector.tensor_tensor(s["root_b"][:], s["root_a"][:], s["var_eps"][:], ALU.mult).then_inc(step, 1)
    reach(dve, step, at + 2)
    nc.vector.tensor_scalar(s["root_c"][:], s["root_b"][:], -0.5, 1.5, ALU.mult, ALU.add).then_inc(step, 1)
    reach(dve, step, at + 3)
    nc.vector.tensor_tensor(s["rstd"][:], s["root_est"][:], s["root_c"][:], ALU.mult).then_inc(step, 1)
    reach(dve, step, at + 4)
    for i in range(TI):
        nc.vector.tensor_scalar(s["res"][:, i, :], s["res"][:, i, :], s["mv"][:, i, 0:1], s["rstd"][:, i:i + 1],
                                ALU.subtract, ALU.mult).then_inc(step, 1)


FF_COLS = {}
_at = 0
for _name, _kt, _cols in (("w1", DT, F), ("w2", DT, F), ("h1", FT, F), ("h2", FT, F), ("w3", FT, D)):
    FF_COLS[_name] = (_at, _kt, _cols)
    _at += _kt * _cols
FF_TOTAL = _at
PIECE = FT * T
PIECES = [(n, at + i, min(PIECE, kt * cols - i)) for n, (at, kt, cols) in FF_COLS.items()
          for i in range(0, kt * cols, PIECE)]


def feed_forward_phase(nc, a, x1, wf, out):
    with ExitStack() as ctx:
        def sb(name, shape, dt=F32):
            return ctx.enter_context(nc.sbuf_tensor("f_" + name, shape, dt))

        def sem(name):
            return ctx.enter_context(nc.semaphore("f_" + name))

        def bank(name):
            return ctx.enter_context(nc.psum_tensor("f_" + name, [P, 512], F32))
        RING = 4
        f_bank = [bank(f"layer_bank{i}") for i in range(RING)]
        turn_bank = [bank(f"turn_bank{i}") for i in range(DT)]
        out_bank = [bank(f"out_bank{i}") for i in range(2)]

        w_all = sb("w_all", [P, FF_TOTAL], F32R)
        w = {n: w_all[:, at:at + kt * cols].rearrange("p (k m) -> p k m", k=kt) for n, (at, kt, cols) in FF_COLS.items()}
        scales = sb("scales", [P, 4, FT])
        s3 = sb("s3", [P, 2, D])
        ident = sb("ident", [P, P])
        ones = sb("ones", [P, 2])
        differ = sb("differ", [P, len(PIECES)])
        inexact = sb("inexact", [1, 2], I32)
        x_turn, x_res = sb("x_turn", [P, TI, D]), sb("x_res", [P, TI, D])
        xt_hi, xt_lo = sb("xt_hi", [P, DT, T], F32R), sb("xt_lo", [P, DT, T], F32R)
        ha_hi, ha_lo = sb("ha_hi", [P, FT, T], F32R), sb("ha_lo", [P, FT, T], F32R)
        hb_hi, hb_lo = sb("hb_hi", [P, FT, T], F32R), sb("hb_lo", [P, FT, T], F32R)
        silu = [sb(f"silu{i}", [P, T]) for i in range(2)]
        h_full = [sb(f"h_full{i}", [P, T]) for i in range(2)]
        res = sb("res", [P, TI, D])
        stats, mv = sb("stats", [P, TI, 6]), sb("mv", [P, TI, 2])
        var_eps, log_var = sb("var_eps", [P, TI]), sb("log_var", [P, TI])
        root_est, root_a, root_b, root_c, rstd = (sb(f"root{i}", [P, TI]) for i in range(5))

        ones_made = sem("ones_made")
        piece_hi, piece_compared = sem("piece_hi"), sem("piece_compared")
        differ_summed, total_made, inexact_made = sem("differ_summed"), sem("total_made"), sem("inexact_made")
        consts_in = sem("consts_in")
        w_in = {n: sem(f"{n}_in") for n in FF_COLS}
        turn_in, res_in = sem("turn_in"), sem("res_in")
        turned = sem("turned")
        turned_hi, turned_lo = sem("turned_hi"), sem("turned_lo")
        LAYER_TILES = 4 * FT
        f_ready = sem("f_ready")
        silu_done, gate_done = sem("silu_done"), sem("gate_done")
        gelu_done = sem("gelu_done")
        h_hi_made, h_split = sem("h_hi_made"), sem("h_split")
        y_ready, y_scaled = sem("y_ready"), sem("y_scaled")
        res_made = sem("res_made")
        ln_step, log_made, rs_made = sem("ln_step"), sem("log_made"), sem("rs_made")
        stored = sem("stored")
        sp_passed, dve_passed = sem("sp_passed"), sem("dve_passed")

        block = ctx.enter_context(nc.Block())

        @block.sync
        def _(sp):
            sp.dma_start(ident[:], a["ident"]).then_inc(consts_in, 16)
            sp.dma_start(scales[:], a["scales"]).then_inc(consts_in, 16)
            for i in range(2):
                sp.dma_start(s3[:, i, :], a["s3"].partition_broadcast(P)).then_inc(consts_in, 16)
            sp.dma_start(x_turn[:], x1[0]).then_inc(turn_in, 16)
            for n, (at, kt, cols) in FF_COLS.items():
                sp.dma_start(w_all[:, at:at + kt * cols].bitcast(F32), wf[:, at:at + kt * cols]).then_inc(w_in[n], 16)
            with sp.Fori(0, BATCH) as c:
                sp.dma_start(x_res[:], x1[c]).then_inc(res_in, 16)
                reach_alone(sp, turned, 2 * c + 2, sp_passed)
                sp.dma_start(x_turn[:], x1[(c + 1) % BATCH]).then_inc(turn_in, 16)
                reach_alone(sp, ln_step, LN_STEPS * c + LN_STEPS, sp_passed)
                sp.dma_start(out[c].rearrange("(i p) d -> p i d", p=P), res[:]).then_inc(stored, 16)
                reach_alone(sp, stored, 16 * c + 16, sp_passed)

        @block.scalar
        def _(act):
            for n, (name, at, cols) in enumerate(PIECES):
                act.wait_ge(w_in[name], 16)
                if n >= 2:
                    act.wait_ge(piece_compared, n - 1)
                hi = (ha_hi, hb_hi)[n % 2][:].rearrange("p k t -> p (k t)")
                nc.scalar.copy(hi[:, 0:cols], w_all[:, at:at + cols].bitcast(F32)).then_inc(piece_hi, 1)
            act.wait_ge(consts_in, 64)

            def turn_hi(c, ct):
                act.wait_ge(turned, 2 * c + ct + 1)
                nc.scalar.copy(xt_hi[:, ct, :], turn_bank[ct][:]).then_inc(turned_hi, 1)

            def gated(c, m):
                act.wait_ge(f_ready, LAYER_TILES * c + 2 * m + 1)
                if m >= 2:
                    act.wait_ge(gate_done, FT * c + m - 1)
                nc.scalar.activation(silu[m % 2][:], f_bank[2 * m % RING][:], ACT.Silu,
                                     scale=scales[:, 0, m:m + 1]).then_inc(silu_done, 1)

            def gate_hi(c, m):
                act.wait_ge(gate_done, FT * c + m + 1)
                nc.scalar.copy(ha_hi[:, m, :], h_full[m % 2][:]).then_inc(h_hi_made, 1)

            def gelu(c, layer, m):
                n = FT * layer + m
                act.wait_ge(f_ready, LAYER_TILES * c + FT + n + 1)
                act.wait_ge(h_split, 3 * FT * c + n - 1)
                nc.scalar.activation(h_full[m % 2][:], f_bank[m % RING][:], ACT.Gelu,
                                     scale=scales[:, 1 + layer, m:m + 1]).then_inc(gelu_done, 1)

            for ct in range(DT):
                turn_hi(0, ct)
            with act.Fori(0, BATCH) as c:
                for m in range(FT):
                    gated(c, m)
                    if m > 0:
                        gate_hi(c, m - 1)
                gate_hi(c, FT - 1)
                for layer in (1, 2):
                    for m in range(FT):
                        gelu(c, layer, m)
                        if layer == 2 and m in (3, 4):
                            turn_hi(c + 1, m - 3)
                act.wait_ge(ln_step, LN_STEPS * c + 2 * TI + 1)
                nc.scalar.activation(log_var[:], var_eps[:], ACT.Ln).then_inc(log_made, 1)
                act.wait_ge(log_made, c + 1)
                nc.scalar.activation(root_est[:], log_var[:], ACT.Exp, scale=-0.5).then_inc(rs_made, 1)

        @block.vector
        def _(dve):
            nc.vector.memset(ones[:], 1.0).then_inc(ones_made, 1)
            for n, (name, at, cols) in enumerate(PIECES):
                dve.wait_ge(piece_hi, n + 1)
                if n >= 2:
                    dve.wait_ge(piece_compared, n - 1)
                hi, flags = (b[n % 2][:].rearrange("p k t -> p (k t)")[:, 0:cols] for b in ((ha_hi, hb_hi), (ha_lo, hb_lo)))
                nc.vector.scalar_tensor_tensor(out=flags, in0=w_all[:, at:at + cols].bitcast(F32), scalar=1.0, in1=hi.bitcast(F32),
                                               op0=ALU.mult, op1=ALU.not_equal,
                                               accum_out=differ[:, n:n + 1]).then_inc(piece_compared, 1)
            dve.wait_ge(differ_summed, 1)
            nc.vector.tensor_reduce(ones[0:1, 0:1], out_bank[0][0:1, 0:len(PIECES)], AX.X, ALU.add).then_inc(total_made, 1)
            dve.wait_ge(total_made, 1)
            nc.vector.tensor_copy(inexact[0:1, 0:1], ones[0:1, 0:1]).then_inc(inexact_made, 1)
            dve.wait_ge(consts_in, 64)

            def turn_lo(c, ct):
                dve.wait_ge(turned_hi, 2 * c + ct + 1)
                nc.vector.tensor_tensor(xt_lo[:, ct, :], turn_bank[ct][:], xt_hi[:, ct, :].bitcast(F32),
                                        ALU.subtract).then_inc(turned_lo, 1)

            def lo(c, n, hi_buf, lo_buf):
                m = n % FT
                dve.wait_ge(h_hi_made, 3 * FT * c + n + 1)
                nc.vector.tensor_tensor(lo_buf[:, m, :], h_full[m % 2][:], hi_buf[:, m, :].bitcast(F32),
                                        ALU.subtract).then_inc(h_split, 1)

            def gate(c, m):
                dve.wait_ge(f_ready, LAYER_TILES * c + 2 * m + 2)
                dve.wait_ge(silu_done, FT * c + m + 1)
                if m >= 2:
                    dve.wait_ge(h_split, 3 * FT * c + m - 1)
                nc.vector.scalar_tensor_tensor(out=h_full[m % 2][:], in0=f_bank[(2 * m + 1) % RING][:],
                                               scalar=scales[:, 1, m:m + 1], in1=silu[m % 2][:],
                                               op0=ALU.mult, op1=ALU.mult).then_inc(gate_done, 1)

            norm = dict(passed=dve_passed, ln_step=ln_step, rs_made=rs_made, res=res, stats=stats, mv=mv, var_eps=var_eps,
                        root_est=root_est, root_a=root_a, root_b=root_b, root_c=root_c, rstd=rstd)
            for ct in range(DT):
                turn_lo(0, ct)
            with dve.Fori(0, BATCH) as c:
                for m in range(FT):
                    gate(c, m)
                    if m > 0:
                        lo(c, m - 1, ha_hi, ha_lo)
                lo(c, FT - 1, ha_hi, ha_lo)
                for layer in (1, 2):
                    hi_buf, lo_buf = ((hb_hi, hb_lo), (ha_hi, ha_lo))[layer - 1]
                    for m in range(FT):
                        dve.wait_ge(gelu_done, 2 * FT * c + FT * (layer - 1) + m + 1)
                        nc.vector.tensor_copy(hi_buf[:, m, :], h_full[m % 2][:]).then_inc(h_hi_made, 1)
                        lo(c, FT * layer + m, hi_buf, lo_buf)
                        if layer == 2 and m in (3, 4):
                            turn_lo(c + 1, m - 3)
                dve.wait_ge(res_in, 16 * c + 16)
                for half in range(2):
                    two = slice(2 * half, 2 * half + 2)
                    dve.wait_ge(y_ready, 2 * c + half + 1)
                    nc.vector.tensor_tensor(res[:, two, :], out_bank[half][:].rearrange("p (i d) -> p i d", i=2), s3[:],
                                            ALU.mult).then_inc(y_scaled, 1)
                for half in range(2):
                    two = slice(2 * half, 2 * half + 2)
                    dve.wait_ge(y_scaled, 2 * c + half + 1)
                    nc.vector.tensor_tensor(res[:, two, :], res[:, two, :], x_res[:, two, :], ALU.add).then_inc(res_made, 1)
                dve.wait_ge(res_made, 2 * c + 2)
                norm_statistics(nc, dve, c, norm)
                norm_apply(nc, dve, c, norm)

        @block.tensor
        def _(pe):
            pe.wait_ge(consts_in, 64)
            pe.wait_ge(ones_made, 1)

            def turn(c):
                pe.wait_ge(turn_in, 16 * c + 16)
                for ct in range(DT):
                    for i in range(TI):
                        mm = nc.tensor.transpose(turn_bank[ct][:, P * i:P * i + P], x_turn[:, i, P * ct:P * ct + P], ident[:])
                    mm.then_inc(turned, 1)

            def layers(dt):
                def both(out, weight, hi, lo, first, last, weight_left=True):
                    for n, half in enumerate((hi, lo)):
                        left, right = (weight, half) if weight_left else (half, weight)
                        mm = nc.tensor.matmul(out, left.bitcast(dt), right.bitcast(dt),
                                              start=first and n == 0, stop=last and n == 1)
                    return mm

                with pe.Fori(0, BATCH) as c:
                    pe.wait_ge(turned_lo, 2 * c + 2)
                    for m in range(FT):
                        for n, name in enumerate(("w1", "w2")):
                            g = 2 * m + n
                            if m >= 2:
                                pe.wait_ge((silu_done, gate_done)[n], FT * c + m - 1)
                            for kt in range(DT):
                                mm = both(f_bank[g % RING][:], w[name][:, kt, P * m:P * m + P],
                                          xt_hi[:, kt, :], xt_lo[:, kt, :], kt == 0, kt == DT - 1)
                            mm.then_inc(f_ready, 1)
                    for layer, (name, hi, lo) in enumerate((("h1", ha_hi, ha_lo), ("h2", hb_hi, hb_lo))):
                        for m in range(FT):
                            n = FT * layer + m
                            if n < RING:
                                pe.wait_ge(gate_done, FT * c + FT - 1 + n // 2)
                            else:
                                pe.wait_ge(gelu_done, 2 * FT * c + n - RING + 1)
                            for kt in range(FT):
                                if m == 0:
                                    pe.wait_ge(h_split, 3 * FT * c + FT * layer + kt + 1)
                                mm = both(f_bank[m % RING][:], w[name][:, kt, P * m:P * m + P],
                                          hi[:, kt, :], lo[:, kt, :], kt == 0, kt == FT - 1)
                            mm.then_inc(f_ready, 1)
                            if layer == 1 and m == 3:
                                pe.wait_ge(turned_lo, 2 * c + 2)
                                turn(c + 1)
                    for i in range(TI):
                        tok = slice(P * i, P * i + P)
                        for kt in range(FT):
                            if i == 0:
                                pe.wait_ge(h_split, 3 * FT * c + 2 * FT + kt + 1)
                            mm = both(out_bank[i // 2][:, D * (i % 2):D * (i % 2) + D], w["w3"][:, kt, :],
                                      ha_hi[:, kt, tok], ha_lo[:, kt, tok], kt == 0, kt == FT - 1, weight_left=False)
                        if i % 2:
                            mm.then_inc(y_ready, 1)

            turn(0)
            pe.wait_ge(piece_compared, len(PIECES))
            nc.tensor.matmul(out_bank[0][0:1, 0:len(PIECES)], ones[:, 1:2], differ[:], start=True,
                             stop=True).then_inc(differ_summed, 1)
            pe.wait_ge(inexact_made, 1)
            bits = pe.value_load(inexact[0:1, 0:1], min_val=0)
            with pe.If(bits == 0):
                layers(F32R)
            with pe.Else():
                layers(F32)


def build(nc, a, out):
    x1 = nc.dram_tensor("x1", [BATCH, P, TI, D], F32, kind="Internal").ap()
    wf = nc.dram_tensor("wf_copy", [P, FF_TOTAL], F32, kind="Internal").ap()
    with nc.semaphore("wf_copied") as wf_copied, nc.Block() as block:
        @block.sync
        def _(sp):
            sp.dma_start(wf, a["wf"]).then_inc(wf_copied, 16)
            sp.wait_ge(wf_copied, 16)
    attention_phase(nc, a, x1)
    feed_forward_phase(nc, a, x1, wf, out)


def kernel(L0_attn_x, L0_attn_w_qkv, L0_attn_w_ky, L0_attn_w_proj, L0_ffn_w1_w, L0_ffn_w1_s, L0_ffn_w2_w,
           L0_ffn_w2_s, L0_ffn_h1_w, L0_ffn_h1_s, L0_ffn_h2_w, L0_ffn_h2_s, L0_ffn_w3_w, L0_ffn_w3_s):
    from concourse import bacc
    from concourse.bass_utils import run_bass_kernel_spmd

    def tiles(w):
        return w.T.reshape(-1, P, w.shape[0]).transpose(1, 0, 2)

    heads = np.arange(D).reshape(2, PAIRS, 2, HD)
    order = heads.transpose(0, 2, 3, 1).reshape(-1)
    wq, wk, wv = (L0_attn_w_qkv[D * i:D * i + D] for i in range(3))
    w4 = np.stack([tiles(w) for w in (wq[order], L0_attn_w_ky[order], wk[order], wv)], axis=2)

    sel = np.zeros((64, P), np.float32)
    for n in range(HU):
        for base in (0, 32):
            sel[base + n, 64 * (n % 2) + n // 2 + PAIRS * np.arange(HD)] = 1

    x = L0_attn_x
    arrays = {
        "xt": x.transpose(0, 2, 1).reshape(BATCH, DT, P, T).transpose(0, 2, 1, 3),
        "xn": x.reshape(BATCH, TI, P, D).transpose(0, 2, 1, 3),
        "w4": w4,
        "wp": tiles(L0_attn_w_proj),
        "ident": np.eye(P, dtype=np.float32),
        "sel": sel,
        "tri": np.stack([np.triu(np.ones((P, P), np.float32)), np.ones((P, P), np.float32)], axis=1),
        "count": np.arange(1, T + 1, dtype=np.float32).reshape(TI, P).T,
        "wf": np.concatenate([tiles(w).reshape(P, -1) for w in
                              (L0_ffn_w1_w, L0_ffn_w2_w, L0_ffn_h1_w, L0_ffn_h2_w, L0_ffn_w3_w)], axis=1),
        "scales": np.stack([s.reshape(FT, P).T for s in
                            (L0_ffn_w1_s, L0_ffn_w2_s, L0_ffn_h1_s, L0_ffn_h2_s)], axis=1),
        "s3": L0_ffn_w3_s,
    }
    arrays = {f"in_{n}": np.ascontiguousarray(v) for n, v in arrays.items()}
    nc = bacc.Bacc("TRN2", target_bir_lowering=False, num_devices=1)
    a = {n[3:]: nc.dram_tensor(n, v.shape, mybir.dt.from_np(v.dtype), kind="ExternalInput").ap() for n, v in arrays.items()}
    out = nc.dram_tensor("out", (BATCH, T, D), F32, kind="ExternalOutput").ap()
    build(nc, a, out)
    return run_bass_kernel_spmd(nc, [arrays], core_ids=[0]).results[0]["out"]
```

```python
import math
from contextlib import ExitStack

import numpy as np

import concourse.bass as bass
from concourse import mybir

F32 = mybir.dt.float32
F32R = mybir.dt.float32r
I32 = mybir.dt.int32
ALU = mybir.AluOpType
ACT = mybir.ActivationFunctionType
AX = mybir.AxisListType

P = 128
BATCH, T, D = 8, 512, 256
H, HD = 16, 16
F = 1024
TI = T // P
DT = D // P
FT = F // P
HU = H // 2
PAIRS = HU // 2
UNITS = 2 * BATCH
COPIES = 4
SW = 32
ONE, EXP = HD, HD + 1
USED = HD + 2
STEPS = PAIRS
LAG = 2
KEY_TILES = ((0, 3), (1, 2))
EPS = 1e-6
LN_EPS = 1e-5
CLIP = 15.0
CHUNKS = 3
W_AT = (0, 512, 1024, 896)
W_COLS = 1280
CHUNK_COLS = ((0, 512), (512, 512), (1024, 256))
STACK_DMAS = 2 * COPIES
LN_STEPS = 3 * TI + 1
ATT_STEPS = 4


class Unit:

    def __init__(self, batch, half):
        self.batch, self.half = batch, half
        self.index = 2 * batch + half

    def shift(self, n):
        half = self.half + n
        return Unit(self.batch + half // 2, half % 2)


FIRST_W = STEPS + LAG


def reach(engine, sem, value):
    if isinstance(value, int) and value <= 0:
        return
    engine.wait_ge(sem, value)


def at_most(value, limit):
    return min(value, limit) if isinstance(value, int) else value


def reach_alone(engine, sem, value, passed):
    reach(engine, sem, value)
    engine.sem_inc(passed, 1)


def attention_phase(nc, a, x1):
    with ExitStack() as ctx:
        def sb(name, shape, dt=F32):
            return ctx.enter_context(nc.sbuf_tensor(name, shape, dt))

        def sem(name):
            return ctx.enter_context(nc.semaphore(name))

        def bank(name):
            return ctx.enter_context(nc.psum_tensor(name, [P, 512], F32))
        y_bank = [bank("y_bank0"), bank("y_bank1")]
        w_bank = [bank("w_bank0"), bank("w_bank1"), bank("w_bank2")]
        acc = bank("acc_bank")
        flip = bank("flip_bank")
        misc = bank("misc_bank")

        w_hi = sb("w_hi", [P, DT, 4, D], F32R)
        w_lo = sb("w_lo", [P, DT, 4, D], F32R)
        wp_hi = sb("wp_hi", [P, DT, D], F32R)
        wp_lo = sb("wp_lo", [P, DT, D], F32R)
        ident = sb("ident", [P, P])
        tri = sb("tri", [P, 2, P])
        count = sb("count", [P, TI])
        sum_exp = sb("sum_exp", [P, SW])
        xt_raw = sb("xt_raw", [P, DT, T])
        xt_hi = sb("xt_hi", [P, DT, T], F32R)
        xt_lo = sb("xt_lo", [P, DT, T], F32R)
        x_nat = sb("x_nat", [P, TI, D])
        q_full = [sb(f"q_full{t}", [P, T]) for t in range(2)]
        q_hi, q_lo = sb("q_hi", [P, T], F32R), sb("q_lo", [P, T], F32R)
        ky_hi, ky_lo = sb("ky_hi", [P, T], F32R), sb("ky_lo", [P, T], F32R)
        k_hi, k_lo = sb("k_hi", [P, T], F32R), sb("k_lo", [P, T], F32R)
        qc_hi, qc_lo = sb("qc_hi", [P, T], F32R), sb("qc_lo", [P, T], F32R)
        q_stack = [sb(f"q_stack{t}", [P, PAIRS, T], F32R) for t in range(2)]
        ky_stack = [sb(f"ky_stack{t}", [P, PAIRS, T], F32R) for t in range(2)]
        k_stack = [sb(f"k_stack{t}", [P, PAIRS, T], F32R) for t in range(2)]
        qc_stack = [sb(f"qc_stack{t}", [P, PAIRS, T], F32R) for t in range(2)]
        v_stage = sb("v_stage", [P, TI, HU, HD])
        v_aug = [sb(f"v_aug{t}", [P, TI, HU, SW]) for t in range(2)]
        RING = 4
        e_ring, w_ring = sb("e_ring", [P, RING, W_COLS]), sb("w_ring", [P, RING, W_COLS])
        e_buf, w_buf = ([ring[:, i, :] for i in range(RING)] for ring in (e_ring, w_ring))
        w_raw = e_ring[:].rearrange("p r c -> p (r c)")[:, 0:DT * 4 * D].rearrange("p (k n c) -> p k n c", k=DT, n=4)
        wp_raw = w_buf[0][:, 0:DT * D].rearrange("p (k c) -> p k c", k=DT)
        acc_copy = sb("acc_copy", [P, T])
        acc_turned = sb("acc_turned", [P, TI, 2, 2, USED])
        agg = [sb(f"agg{t}", [P, TI, HU]) for t in range(2)]
        agg_eps = sb("agg_eps", [P, TI, 2 * HU])
        c_cols = sb("c_cols", [P, TI, 2 * HU])
        c_spread = sb("c_spread", [P, TI, 2, HD, PAIRS])
        att_raw = sb("att_raw", [P, TI, H, HD + 1])
        base = sb("base", [P, TI, H])
        v_sum = sb("v_sum", [P, TI, H, HD])
        base_v = sb("base_v", [P, TI, H, HD])
        base_sum = sb("base_sum", [P, TI, H])
        att_den = sb("att_den", [P, TI * H])
        att_inv = sb("att_inv", [P, TI * H])
        att = sb("att", [P, TI, D])
        att_hi, att_lo = sb("att_hi", [P, DT, T], F32R), sb("att_lo", [P, DT, T], F32R)
        res = sb("res", [P, TI, D])
        stats, mv = sb("stats", [P, TI, 6]), sb("mv", [P, TI, 2])
        var_eps, rstd, minus_half = sb("var_eps", [P, TI]), sb("rstd", [P, TI]), sb("minus_half", [P, TI])

        acc_zeroed = sem("acc_zeroed")
        made_once = sem("made_once")
        weights_in = sem("weights_in")
        weights_split = sem("weights_split")
        xt_in = sem("xt_in")
        xn_in = sem("xn_in")
        xt_split = sem("xt_split")
        xt_hi_made = sem("xt_hi_made")
        k_ready, v_ready = sem("k_ready"), sem("v_ready")
        q_ready, ky_ready = sem("q_ready"), sem("ky_ready")
        k_hi_made, k_lo_made = sem("k_hi_made"), sem("k_lo_made")
        q_hi_made, q_lo_made = sem("q_hi_made"), sem("q_lo_made")
        ky_hi_made, ky_lo_made = sem("ky_hi_made"), sem("ky_lo_made")
        v_staged, v_spread = sem("v_staged"), sem("v_spread")
        q_stacked = [sem(f"q_stacked{t}") for t in range(2)]
        ky_stacked = [sem(f"ky_stacked{t}") for t in range(2)]
        k_stacked = [sem(f"k_stacked{t}") for t in range(2)]
        qc_stacked = [sem(f"qc_stacked{t}") for t in range(2)]
        y_scores = sem("y_scores")
        exp_done = sem("exp_done")
        e_clipped = sem("e_clipped")
        e_masked = sem("e_masked")
        w_scores = sem("w_scores")
        abs_done = sem("abs_done")
        ln_done = sem("ln_done")
        w_masked = sem("w_masked")
        exp_summed, acc_done = sem("exp_summed"), sem("acc_done")
        acc_copied = sem("acc_copied")
        acc_flipped = sem("acc_flipped")
        acc_kept = sem("acc_kept")
        agg_added, att_added = sem("agg_added"), sem("att_added")
        cols_step = sem("cols_step")
        spread_ready = sem("spread_ready")
        qc_made = sem("qc_made")
        qc_hi_made, qc_lo_made = sem("qc_hi_made"), sem("qc_lo_made")
        base_made = sem("base_made")
        v_sum_ready, v_sum_copied = sem("v_sum_ready"), sem("v_sum_copied")
        base_step = sem("base_step")
        att_step = sem("att_step")
        turned = sem("turned")
        turned_hi, turned_lo = sem("turned_hi"), sem("turned_lo")
        proj_ready = sem("proj_ready")
        res_made = sem("res_made")
        ln_step = sem("ln_step")
        root_made = sem("root_made")
        x1_stored = sem("x1_stored")
        pool_passed, sp_passed, dve_passed = sem("pool_passed"), sem("sp_passed"), sem("dve_passed")

        norm_tiles = dict(passed=dve_passed, ln_step=ln_step, root_made=root_made, res=res, stats=stats, mv=mv, var_eps=var_eps,
                          minus_half=minus_half, rstd=rstd)
        rows = [slice(64 * par, 64 * par + 64) for par in range(2)]
        block = ctx.enter_context(nc.Block())

        def tiles_of(c):
            return (((0, 0),), ((0, 1), (384, 3)), ((0, 2),))[c]

        def weights_of(k, s):
            return (k.shift(-2), s + LAG) if s < LAG else (k.shift(-1), s - LAG)

        def step_of(u, m):
            return STEPS * (u.index + 1) + LAG + m

        ALL, NONE = (0, 1, 2, 3), ()

        def run(slot, fori):
            slot(Unit(0, 0), w=NONE, before=(False, False))
            slot(Unit(0, 1), w=(2, 3), before=(True, False), x=1)
            slot(Unit(1, 0))
            slot(Unit(1, 1), x=2, divide=0)
            with fori(2, BATCH - 1) as j:
                slot(Unit(j, 0), out=j - 2, first_in_loop=True)
                slot(Unit(j, 1), x=j + 1, divide=j - 1, norm=j - 2)
            slot(Unit(BATCH - 1, 0), out=BATCH - 3, first_in_loop=True)
            slot(Unit(BATCH - 1, 1), project=False, divide=BATCH - 2, norm=BATCH - 3)
            slot(Unit(BATCH, 0), y=False, project=False, out=BATCH - 2)
            slot(Unit(BATCH, 1), y=False, project=False, w=(0, 1), before=(False, True), divide=BATCH - 1, norm=BATCH - 2)
            slot(Unit(BATCH + 1, 0), y=False, project=False, w=NONE, before=(False, False), out=BATCH - 1)
            slot(Unit(BATCH + 1, 1), y=False, project=False, w=NONE, before=(False, False), norm=BATCH - 1)

        def sums_of(s, y, w, before):
            return before if s == 0 else (y, s - 1 in w)

        @block.sync
        def _(sp):
            sp.dma_start(w_raw, a["w4"]).then_inc(weights_in, 16)
            sp.dma_start(xt_raw[:], a["xt"][0]).then_inc(xt_in, 16)
            sp.dma_start(ident[:], a["ident"]).then_inc(weights_in, 16)
            sp.dma_start(wp_raw, a["wp"]).then_inc(weights_in, 16)
            sp.dma_start(tri[:], a["tri"]).then_inc(weights_in, 16)
            sp.dma_start(count[:], a["count"]).then_inc(weights_in, 16)

            def stack(dst, hi, lo, copies, sem):
                for par in range(2):
                    for r, half in enumerate(copies):
                        src = (hi, lo)[half][64 * par:64 * par + 64, :]
                        to = dst[64 * par + HD * r:64 * par + HD * r + HD, :, :]
                        sp.dma_start(to.bitcast(F32), src.bitcast(F32)).then_inc(sem, 16)
            LEFT, RIGHT = (0, 0, 1, 1), (0, 1, 0, 1)

            def stack_q(u):
                reach(sp, q_hi_made, u.index + 1)
                reach_alone(sp, q_lo_made, u.index + 1, sp_passed)
                reach(sp, y_scores, 24 * (u.index - 1))
                stack(q_stack[u.half], q_hi, q_lo, RIGHT, q_stacked[u.half])

            def stack_ky(u):
                reach(sp, ky_hi_made, u.index + 1)
                reach_alone(sp, ky_lo_made, u.index + 1, sp_passed)
                reach(sp, y_scores, 24 * (u.index - 1))
                stack(ky_stack[u.half], ky_hi, ky_lo, LEFT, ky_stacked[u.half])

            def stack_qc(v):
                reach(sp, qc_hi_made, v.index + 1)
                reach_alone(sp, qc_lo_made, v.index + 1, sp_passed)
                reach(sp, w_scores, 24 * (v.index - 1))
                stack(qc_stack[v.half], qc_hi, qc_lo, RIGHT, qc_stacked[v.half])

            def stack_k(u):
                reach(sp, k_hi_made, u.index + 1)
                reach_alone(sp, k_lo_made, u.index + 1, sp_passed)
                reach(sp, w_scores, 24 * (u.index - 1))
                stack(k_stack[u.half], k_hi, k_lo, LEFT, k_stacked[u.half])

            def slot(k, y=True, project=True, w=ALL, x=None, divide=None, out=None, norm=None, **_):
                if x is not None:
                    reach_alone(sp, xt_split, x, sp_passed)
                    if isinstance(x, int):
                        if x < BATCH:
                            sp.dma_start(xt_raw[:], a["xt"][x]).then_inc(xt_in, 16)
                    else:
                        sp.dma_start(xt_raw[:], a["xt"][x]).then_inc(xt_in, 16)
                if out is not None:
                    reach_alone(sp, res_made, 2 * out, sp_passed)
                    sp.dma_start(x_nat[:], a["xn"][out]).then_inc(xn_in, 16)
                if project:
                    stack_ky(k.shift(1))
                if 2 in w:
                    stack_qc(k.shift(-1))
                if project:
                    stack_q(k.shift(1))
                if y:
                    stack_k(k)
                if norm is not None:
                    reach_alone(sp, ln_step, LN_STEPS * (norm + 1), sp_passed)
                    sp.dma_start(x1[norm], res[:]).then_inc(x1_stored, 16)

            stack_q(Unit(0, 0))
            stack_ky(Unit(0, 0))
            run(slot, sp.Fori)
            sp.wait_ge(x1_stored, 16 * BATCH)

        @block.gpsimd
        def _(pool):
            for t in range(2):
                nc.gpsimd.memset(v_aug[t][:, :, :, HD:SW], 0.0)
            nc.gpsimd.memset(minus_half[:], -0.5)
            nc.gpsimd.memset(sum_exp[:], 0.0).then_inc(made_once, 1)
            pool.wait_ge(made_once, 1)
            for t in range(2):
                nc.gpsimd.memset(v_aug[t][:, :, :, ONE:ONE + 1], 1.0)
            nc.gpsimd.memset(sum_exp[:, EXP:EXP + 1], 1.0).then_inc(made_once, 1)

            def mask(buf, done):
                for blocks in (buf[:, 0:1024].rearrange("p (b c) -> p b c", b=2)[:, :, 0:P],
                               buf[:, 896:1152].rearrange("p (b c) -> p b c", b=2)):
                    nc.gpsimd.affine_select(out=blocks, in_=blocks, compare_op=ALU.is_ge, fill=0.0, base=0,
                                            pattern=[[0, 2], [1, P]], channel_multiplier=-1).then_inc(done, 1)

            def mask_e(k, n):
                reach_alone(pool, e_clipped, HU * k.index + n + 1, pool_passed)
                mask(e_buf[n % RING], e_masked)

            def mask_w(u, n):
                reach_alone(pool, ln_done, HU * u.index + n + 1, pool_passed)
                mask(w_buf[n % RING], w_masked)

            def spread_values(u):
                reach(pool, v_staged, u.index + 1)
                reach_alone(pool, acc_done, step_of(u.shift(-2), PAIRS - 1) + 1, pool_passed)
                nc.gpsimd.tensor_copy(v_aug[u.half][:, :, :, 0:HD], v_stage[:]).then_inc(v_spread, 1)

            def base_times(b):
                reach(pool, v_sum_copied, 2 * (b + 1))
                reach(pool, base_made, 2 * (b + 1))
                reach(pool, att_step, ATT_STEPS * b)
                nc.gpsimd.tensor_tensor(base_v[:].rearrange("p i h d -> p (i h) d"), v_sum[:].rearrange("p i h d -> p (i h) d"),
                                        base[:].rearrange("p i h -> p (i h)").unsqueeze(2).to_broadcast([P, TI * H, HD]),
                                        ALU.mult).then_inc(base_step, 1)
                nc.gpsimd.tensor_tensor(base_sum[:], base[:], count[:].unsqueeze(2).to_broadcast([P, TI, H]),
                                        ALU.mult).then_inc(base_step, 1)

            def keep_sums(k, s, y, w):
                reach(pool, acc_kept, STEPS * k.index + s + 1)
                if y:
                    nc.gpsimd.tensor_tensor(agg[k.half][:, :, 2 * s:2 * s + 2], acc_turned[:, :, :, 0, EXP],
                                            acc_turned[:, :, :, 1, EXP], ALU.add).then_inc(agg_added, 1)
                if w:
                    u, m = weights_of(k, s)
                    if m == 0 and u.half == 0:
                        reach(pool, att_step, ATT_STEPS * (u.batch - 1) + 2)
                    h = HU * u.half + 2 * m
                    nc.gpsimd.tensor_tensor(att_raw[:, :, h:h + 2, :], acc_turned[:, :, :, 0, 0:HD + 1],
                                            acc_turned[:, :, :, 1, 0:HD + 1], ALU.add).then_inc(att_added, 1)

            def slot(k, y=True, w=ALL, before=(True, True), divide=None, norm=None, **_):
                for s in range(STEPS):
                    sums = sums_of(s, y, w, before)
                    summed = (k, s - 1) if s else (k.shift(-1), STEPS - 1)
                    for par in range(2):
                        if y:
                            mask_e(k, 2 * s + par)
                        if par == 0 and sums[1]:
                            u, m = weights_of(*summed)
                            mask_w(u, 2 * m + 1)
                        if par == 1 and s in w:
                            u, m = weights_of(k, s)
                            mask_w(u, 2 * m)
                        if par == 0 and s == 3 and y:
                            spread_values(k)
                        if par == 0 and s == 0 and divide is not None:
                            base_times(divide)
                        if par == 0 and s == 0 and norm is not None:
                            norm_root(nc, pool, norm, norm_tiles)
                    if any(sums):
                        keep_sums(*summed, *sums)
            run(slot, pool.Fori)

        @block.scalar
        def _(act):
            nc.scalar.preload_act_table_set("natural_log_exp_and_others")
            act.wait_ge(weights_in, 80)
            nc.scalar.copy(w_hi[:], w_raw).then_inc(weights_split, 1)
            nc.scalar.copy(wp_hi[:], wp_raw).then_inc(weights_split, 1)

            def split_x(b):
                reach(act, xt_in, 16 * (b + 1))
                reach(act, v_ready, 2 * b)
                nc.scalar.copy(xt_hi[:], xt_raw[:]).then_inc(xt_hi_made, 1)

            def stack_free(stacked, u):
                reach(act, stacked[u.half], 16 * STACK_DMAS * (u.batch + 1))

            def q_split(u):
                reach(act, q_ready, u.index + 1)
                reach(act, qc_hi_made, u.index - 1)
                reach(act, qc_lo_made, u.index - 1)
                nc.scalar.mul(q_full[u.half][:], misc[:], HD ** -0.5)
                stack_free(q_stacked, u.shift(-1))
                nc.scalar.mul(q_hi[:], misc[:], HD ** -0.5).then_inc(q_hi_made, 1)

            def ky_split(u):
                reach(act, ky_ready, u.index + 1)
                stack_free(ky_stacked, u.shift(-1))
                nc.scalar.copy(ky_hi[:], misc[:]).then_inc(ky_hi_made, 1)

            def k_split(u):
                reach(act, k_ready, u.index + 1)
                stack_free(k_stacked, u.shift(-1))
                nc.scalar.copy(k_hi[:], misc[:]).then_inc(k_hi_made, 1)

            def v_copy(u):
                reach(act, v_ready, u.index + 1)
                reach(act, v_spread, u.index)
                nc.scalar.copy(v_stage[:].rearrange("p i h d -> p (i h d)"), misc[:]).then_inc(v_staged, 1)

            def exps(k, s, par):
                n = 2 * s + par
                reach(act, acc_done, STEPS * k.index + s - 1)
                for c, (at, cols) in enumerate(CHUNK_COLS):
                    reach(act, y_scores, 24 * k.index + 3 * n + c + 1)
                    nc.scalar.activation(e_buf[n % RING][:, at:at + cols], y_bank[(3 * n + c) % 2][:, 0:cols], ACT.Exp).then_inc(exp_done, 1)

            def logs(u, m, par):
                n = 2 * m + par
                reach(act, abs_done, 24 * u.index + 3 * n + 3)
                nc.scalar.activation(w_buf[n % RING], w_buf[n % RING], ACT.Ln, bias=1.0).then_inc(ln_done, 1)

            def qc_split(v):
                reach(act, qc_made, v.index + 1)
                stack_free(qc_stacked, v.shift(-1))
                nc.scalar.copy(qc_hi[:], q_full[v.half][:]).then_inc(qc_hi_made, 1)

            def base_make(v):
                reach(act, cols_step, 5 * v.index + 3)
                if v.half == 0:
                    reach(act, base_step, 2 * v.batch)
                nc.scalar.activation(base[:, :, HU * v.half:HU * v.half + HU], c_cols[:, :, HU:2 * HU], ACT.Ln,
                                     bias=1.0, scale=EPS).then_inc(base_made, 1)

            def v_sum_copy(v):
                reach(act, v_sum_ready, v.index + 1)
                if v.half == 0:
                    reach(act, base_step, 2 * v.batch)
                nc.scalar.copy(v_sum[:, :, HU * v.half:HU * v.half + HU, :],
                               misc[:].rearrange("p (i h d) -> p i h d", i=TI, h=HU)).then_inc(v_sum_copied, 1)

            def turn_hi(b, ct):
                reach(act, turned, 2 * b + ct + 1)
                nc.scalar.copy(att_hi[:, ct, :], misc[:]).then_inc(turned_hi, 1)

            def copy_sums(step):
                reach(act, acc_done, step + 1)
                reach(act, acc_flipped, step)
                nc.scalar.copy(acc_copy[:], acc[:]).then_inc(acc_copied, 1)

            def keep_flipped(step, agg_count, att_count):
                reach(act, acc_flipped, step + 1)
                reach(act, agg_added, agg_count)
                reach(act, att_added, att_count)
                nc.scalar.copy(acc_turned[:].rearrange("p i r g c -> p i (r g) c"),
                               flip[:].rearrange("p (i g c) -> p i g c", i=TI, c=SW)[:, :, :, 0:USED]).then_inc(acc_kept, 1)

            def slot(k, y=True, project=True, w=ALL, before=(True, True), x=None, out=None, norm=None, **_):
                for s in range(STEPS):
                    step = STEPS * k.index + s
                    sums = sums_of(s, y, w, before)
                    summed = (k, s - 1) if s else (k.shift(-1), STEPS - 1)
                    if y:
                        exps(k, s, 0)
                    if s == 0 and out is not None:
                        turn_hi(out, 0)
                    if s == 2 and 2 in w:
                        v_sum_copy(k.shift(-1))
                    if sums[1]:
                        logs(*weights_of(*summed), 1)
                    if s == 0 and x is not None:
                        split_x(x)
                    if s == 0 and out is not None:
                        turn_hi(out, 1)
                    if s == 1 and 2 in w:
                        base_make(k.shift(-1))
                        qc_split(k.shift(-1))
                    if y:
                        exps(k, s, 1)
                    if s in w:
                        logs(*weights_of(k, s), 0)
                    if any(sums):
                        copy_sums(step - 1)
                    if project:
                        (ky_split, q_split, k_split, v_copy)[s](k.shift(1))
                    if any(sums):
                        keep_flipped(step - 1, at_most(step - 1, UNITS * PAIRS), at_most(step - 1 - FIRST_W, UNITS * PAIRS))

            split_x(0)
            for split in (q_split, ky_split, k_split, v_copy):
                split(Unit(0, 0))
            run(slot, act.Fori)

        @block.vector
        def _(dve):
            nc.vector.memset(acc[:, 0:P], 0.0).then_inc(acc_zeroed, 1)
            dve.wait_ge(weights_in, 80)
            dve.wait_ge(weights_split, 2)
            nc.vector.tensor_tensor(w_lo[:], w_raw, w_hi[:].bitcast(F32), ALU.subtract).then_inc(weights_split, 1)
            nc.vector.tensor_tensor(wp_lo[:], wp_raw, wp_hi[:].bitcast(F32), ALU.subtract).then_inc(weights_split, 1)

            def split_x(b):
                reach(dve, xt_hi_made, b + 1)
                nc.vector.tensor_tensor(xt_lo[:], xt_raw[:], xt_hi[:].bitcast(F32), ALU.subtract).then_inc(xt_split, 1)

            def lo_of(lo, hi, made, count, then, scale=1.0):
                reach(dve, made, count)
                nc.vector.scalar_tensor_tensor(out=lo, in0=misc[:], scalar=scale, in1=hi.bitcast(F32),
                                               op0=ALU.mult, op1=ALU.subtract).then_inc(then, 1)

            def stack_free(stacked, u):
                reach(dve, stacked[u.half], 16 * STACK_DMAS * (u.batch + 1))

            def q_split(u):
                stack_free(q_stacked, u.shift(-1))
                lo_of(q_lo[:], q_hi[:], q_hi_made, u.index + 1, q_lo_made, HD ** -0.5)

            def ky_split(u):
                stack_free(ky_stacked, u.shift(-1))
                lo_of(ky_lo[:], ky_hi[:], ky_hi_made, u.index + 1, ky_lo_made)

            def k_split(u):
                stack_free(k_stacked, u.shift(-1))
                lo_of(k_lo[:], k_hi[:], k_hi_made, u.index + 1, k_lo_made)

            def clip(k, n):
                reach(dve, exp_done, 24 * k.index + 3 * n + 3)
                nc.vector.tensor_scalar(e_buf[n % RING], e_buf[n % RING], math.exp(CLIP), math.exp(-CLIP),
                                        ALU.min, ALU.max).then_inc(e_clipped, 1)

            def absolute(k, s, par):
                u, m = weights_of(k, s)
                n = 2 * m + par
                reach(dve, acc_done, STEPS * k.index + s - 1)
                for c, (at, cols) in enumerate(CHUNK_COLS):
                    reach(dve, w_scores, 24 * u.index + 3 * n + c + 1)
                    nc.vector.tensor_scalar(w_buf[n % RING][:, at:at + cols].bitcast(I32), w_bank[c][:, 0:cols].bitcast(I32),
                                            0x7FFFFFFF, None, ALU.bitwise_and).then_inc(abs_done, 1)

            def factors(v):
                start = 5 * v.index
                reach(dve, agg_added, PAIRS * (v.index + 1))
                reach(dve, base_made, v.index)
                reach(dve, spread_ready, v.index)
                nc.vector.tensor_scalar(agg_eps[:, :, HU:2 * HU], agg[v.half][:], EPS, EPS, ALU.add, ALU.add).then_inc(cols_step, 1)
                reach(dve, cols_step, start + 1)
                nc.vector.tensor_scalar(agg_eps[:, :, 0:HU], agg_eps[:, :, HU:2 * HU], EPS, None, ALU.add).then_inc(cols_step, 1)
                reach(dve, cols_step, start + 2)
                nc.vector.reciprocal(c_cols[:], agg_eps[:]).then_inc(cols_step, 1)
                reach(dve, cols_step, start + 3)
                for par in range(2):
                    c = c_cols[:, :, 0:HU].rearrange("p i (q r) -> p i q r", r=2)[:, :, :, par]
                    nc.vector.tensor_copy(c_spread[:, :, par, :, :],
                                          c.unsqueeze(2).to_broadcast([P, TI, HD, PAIRS])).then_inc(cols_step, 1)

            def scale_q(v):
                reach(dve, spread_ready, v.index + 1)
                nc.vector.tensor_tensor(q_full[v.half][:], misc[:], q_full[v.half][:], ALU.mult).then_inc(qc_made, 1)
                stack_free(qc_stacked, v.shift(-1))
                reach(dve, qc_hi_made, v.index + 1)
                reach(dve, qc_made, v.index + 1)
                nc.vector.tensor_tensor(qc_lo[:], q_full[v.half][:], qc_hi[:].bitcast(F32), ALU.subtract).then_inc(qc_lo_made, 1)

            def normalise(b):
                start = ATT_STEPS * b
                reach(dve, att_added, 2 * PAIRS * (b + 1))
                reach(dve, base_step, 2 * (b + 1))
                reach(dve, turned, 2 * b)
                raw = att_raw[:].rearrange("p i h c -> p (i h) c")
                sums = base_v[:].rearrange("p i h d -> p (i h) d")
                nc.vector.scalar_tensor_tensor(out=att_den[:], in0=raw[:, :, ONE], scalar=EPS,
                                               in1=base_sum[:].rearrange("p i h -> p (i h)"),
                                               op0=ALU.add, op1=ALU.add).then_inc(att_step, 1)
                nc.vector.tensor_tensor(sums, sums, raw[:, :, 0:HD], ALU.add).then_inc(att_step, 1)
                reach(dve, att_step, start + 2)
                nc.vector.reciprocal(att_inv[:], att_den[:]).then_inc(att_step, 1)
                reach(dve, att_step, start + 3)
                nc.vector.tensor_tensor(att[:].rearrange("p i (h d) -> p (i h) d", h=H), sums,
                                        att_inv[:].unsqueeze(2).to_broadcast([P, TI * H, HD]), ALU.mult).then_inc(att_step, 1)

            def residual(b, half):
                reach(dve, xn_in, 16 * (b + 1))
                reach(dve, x1_stored, 16 * b)
                reach(dve, proj_ready, 2 * b + half + 1)
                two = slice(2 * half, 2 * half + 2)
                nc.vector.tensor_tensor(res[:, two, :], misc[:].rearrange("p (i d) -> p i d", i=2), x_nat[:, two, :],
                                        ALU.add).then_inc(res_made, 1)

            def turn_lo(b, ct):
                lo_of(att_lo[:, ct, :], att_hi[:, ct, :], turned_hi, 2 * b + ct + 1, turned_lo)

            def slot(k, y=True, project=True, w=ALL, x=None, divide=None, out=None, norm=None, **_):
                for s in range(STEPS):
                    if s == 1 and 2 in w:
                        factors(k.shift(-1))
                    if y:
                        clip(k, 2 * s)
                    if s == 0 and out is not None:
                        turn_lo(out, 0)
                    if s in w:
                        absolute(k, s, 0)
                    if s == 0 and out is not None:
                        turn_lo(out, 1)
                    if s == 0 and x is not None:
                        split_x(x)
                    if s == 1 and 2 in w:
                        scale_q(k.shift(-1))
                    if s in (2, 3) and out is not None:
                        residual(out, s - 2)
                    if y:
                        clip(k, 2 * s + 1)
                    if s in w:
                        absolute(k, s, 1)
                    if s == 1 and norm is not None:
                        norm_apply(nc, dve, norm, norm_tiles)
                    if s == 3 and divide is not None:
                        normalise(divide)
                    if s == 3 and out is not None:
                        reach(dve, res_made, 2 * out + 2)
                        norm_statistics(nc, dve, out, norm_tiles)
                    if project and s < 3:
                        (ky_split, q_split, k_split)[s](k.shift(1))

            split_x(0)
            for split in (q_split, ky_split, k_split):
                split(Unit(0, 0))
            run(slot, dve.Fori)

        @block.tensor
        def _(pe):
            misc_readers = []

            def take_misc(*readers):
                for s, count in misc_readers:
                    reach(pe, s, count)
                misc_readers[:] = readers

            def three(out, left, right, first, last):
                (lh, ll), (rh, rl) = left, right
                nc.tensor.matmul(out, lh, rh, start=first, stop=False)
                nc.tensor.matmul(out, ll, rh, start=False, stop=False)
                return nc.tensor.matmul(out, lh, rl, start=False, stop=last)

            def project_t(u, kind, done):
                reach(pe, xt_split, u.batch + 1)
                m = slice(P * u.half, P * u.half + P)
                for kt in range(DT):
                    mm = three(misc[:], (w_hi[:, kt, kind, m], w_lo[:, kt, kind, m]),
                               (xt_hi[:, kt, :], xt_lo[:, kt, :]), kt == 0, kt == DT - 1)
                mm.then_inc(done, 1)

            def q_proj(u):
                take_misc((q_lo_made, u.index + 1))
                project_t(u, 0, q_ready)

            def ky_proj(u):
                take_misc((ky_lo_made, u.index + 1))
                project_t(u, 1, ky_ready)

            def k_proj(u):
                take_misc((k_lo_made, u.index + 1))
                project_t(u, 2, k_ready)

            def v_proj(u):
                take_misc((v_staged, u.index + 1))
                m = slice(P * u.half, P * u.half + P)
                for i in range(TI):
                    tok = slice(P * i, P * i + P)
                    for kt in range(DT):
                        mm = three(misc[:, tok], (xt_hi[:, kt, tok], xt_lo[:, kt, tok]),
                                   (w_hi[:, kt, 3, m], w_lo[:, kt, 3, m]), kt == 0, kt == DT - 1)
                mm.then_inc(v_ready, 1)

            def chunk(out, left, right, u, n, c):
                r, p = rows[n % 2], n // 2
                for at, j in tiles_of(c):
                    mm = nc.tensor.matmul(out[:, at:at + T - P * j], left[u.half][r, p, P * j:P * j + P],
                                          right[u.half][r, p, P * j:T], start=True, stop=True)
                return mm

            def scores_y(k, n, c):
                if n == 0 and c == 0:
                    reach(pe, q_stacked[k.half], 16 * STACK_DMAS * (k.batch + 1))
                    reach(pe, ky_stacked[k.half], 16 * STACK_DMAS * (k.batch + 1))
                g = 3 * n + c
                reach(pe, exp_done, 24 * k.index + g - 1)
                chunk(y_bank[g % 2], ky_stack, q_stack, k, n, c).then_inc(y_scores, 1)

            def scores_w(u, n, c):
                if n == 0 and c == 0:
                    reach(pe, k_stacked[u.half], 16 * STACK_DMAS * (u.batch + 1))
                    reach(pe, qc_stacked[u.half], 16 * STACK_DMAS * (u.batch + 1))
                reach(pe, abs_done, 24 * u.index + 3 * (n - 1) + c + 1)
                chunk(w_bank[c], k_stack, qc_stack, u, n, c).then_inc(w_scores, 1)

            def scores(k, s, par, y, w):
                for c in range(CHUNKS - 1):
                    if y:
                        scores_y(k, 2 * s + par, c)
                if w:
                    u, m = weights_of(k, s)
                    for c in range(CHUNKS):
                        scores_w(u, 2 * m + par, c)
                if y:
                    scores_y(k, 2 * s + par, CHUNKS - 1)

            def sum_keys(of, stationary, first, last):
                for turn, _ in enumerate(KEY_TILES[0]):
                    for par in range(2):
                        for g, key_tiles in enumerate(KEY_TILES):
                            j = key_tiles[turn]
                            at = SW * (2 * par + g)
                            mm = nc.tensor.matmul(acc[at:at + SW, P * j:T], stationary(j, par),
                                                  of(par)[:, W_AT[j]:W_AT[j] + T - P * j],
                                                  start=first and turn == 0, stop=last and turn == 1)
                return mm

            def sum_exps(k, s, alone):
                step = STEPS * k.index + s
                reach(pe, e_masked, 2 * (HU * k.index + 2 * s + 2))
                reach(pe, acc_copied, step)
                mm = sum_keys(lambda par: e_buf[(2 * s + par) % RING], lambda j, par: sum_exp[:], True, alone)
                if alone:
                    mm.then_inc(acc_done, 1)

            def sum_weights(k, s, alone):
                u, m = weights_of(k, s)
                step = STEPS * k.index + s
                reach(pe, w_masked, 2 * (HU * u.index + 2 * m + 2))
                reach(pe, acc_copied, step)
                reach(pe, v_spread, u.index + 1)
                sum_keys(lambda par: w_buf[(2 * m + par) % RING], lambda j, par: v_aug[u.half][:, j, 2 * m + par, :],
                         alone, True).then_inc(acc_done, 1)

            def flip_sums(step):
                reach(pe, acc_kept, step)
                reach(pe, acc_copied, step + 1)
                for i in range(TI):
                    mm = nc.tensor.transpose(flip[:, P * i:P * i + P], acc_copy[:, P * i:P * i + P], ident[:])
                mm.then_inc(acc_flipped, 1)

            def spread_c(v):
                take_misc((qc_made, v.index + 1))
                reach(pe, cols_step, 5 * (v.index + 1))
                for i in range(TI):
                    mm = nc.tensor.transpose(misc[:, P * i:P * i + P],
                                             c_spread[:, i, :, :, :].rearrange("p r d q -> p (r d q)"), ident[:])
                mm.then_inc(spread_ready, 1)

            def sum_values(v):
                take_misc((v_sum_copied, v.index + 1))
                reach(pe, v_spread, v.index + 1)
                out = misc[:].rearrange("p (i h d) -> p i h d", i=TI, h=HU)
                values = v_aug[v.half][:, :, :, 0:HD]
                mm = nc.tensor.matmul(misc[:], tri[:, 0, :], values.rearrange("p i h d -> p (i h) d"), start=True, stop=False)
                for i in range(1, TI):
                    for j in range(i):
                        mm = nc.tensor.matmul(misc[:, P * i:P * i + P], tri[:, 1, :], v_aug[v.half][:, j, :, 0:HD],
                                              start=False, stop=(i == TI - 1 and j == i - 1))
                mm.then_inc(v_sum_ready, 1)

            def turn(b, ct):
                take_misc((turned_lo, 2 * b + ct + 1))
                reach(pe, att_step, ATT_STEPS * (b + 1))
                for i in range(TI):
                    mm = nc.tensor.transpose(misc[:, P * i:P * i + P], att[:, i, P * ct:P * ct + P], ident[:])
                mm.then_inc(turned, 1)

            def project_out(b, half):
                take_misc((res_made, 2 * b + half + 1))
                reach(pe, turned_lo, 2 * (b + 1))
                for i2 in range(2):
                    i = 2 * half + i2
                    tok = slice(P * i, P * i + P)
                    for ct in range(DT):
                        mm = three(misc[:, D * i2:D * i2 + D], (att_hi[:, ct, tok], att_lo[:, ct, tok]),
                                   (wp_hi[:, ct, :], wp_lo[:, ct, :]), ct == 0, ct == DT - 1)
                mm.then_inc(proj_ready, 1)

            def slot(k, y=True, project=True, w=ALL, before=(True, True), out=None, first_in_loop=False, **_):
                if first_in_loop:
                    misc_readers[:] = [(v_staged, k.index + 1)]
                for s in range(STEPS):
                    sums = sums_of(s, y, w, before)
                    summed = (k, s - 1) if s else (k.shift(-1), STEPS - 1)
                    scores(k, s, 0, y, s in w)
                    if s == 0 and out is not None:
                        turn(out, 0)
                    if s == 2 and 2 in w:
                        sum_values(k.shift(-1))
                    if sums[0]:
                        sum_exps(*summed, not sums[1])
                    if s == 0 and out is not None:
                        turn(out, 1)
                    if s == 1 and 2 in w:
                        spread_c(k.shift(-1))
                    if s in (2, 3) and out is not None:
                        project_out(out, s - 2)
                    scores(k, s, 1, y, s in w)
                    if sums[1]:
                        sum_weights(*summed, not sums[0])
                    if project:
                        (ky_proj, q_proj, k_proj, v_proj)[s](k.shift(1))
                    if any(sums):
                        flip_sums(STEPS * k.index + s - 1)

            pe.wait_ge(weights_split, 4)
            pe.wait_ge(made_once, 2)
            pe.wait_ge(acc_zeroed, 1)
            for proj in (q_proj, ky_proj, k_proj, v_proj):
                proj(Unit(0, 0))
            run(slot, pe.Fori)


def norm_statistics(nc, dve, b, s):
    base = LN_STEPS * b
    for i in range(TI):
        nc.vector.bn_stats(s["stats"][:, i, :], s["res"][:, i, :]).then_inc(s["ln_step"], 1)
    reach_alone(dve, s["ln_step"], base + TI, s["passed"])
    for i in range(TI):
        nc.vector.bn_aggr(s["mv"][:, i, :], s["stats"][:, i, :]).then_inc(s["ln_step"], 1)
    reach(dve, s["ln_step"], base + 2 * TI)
    nc.vector.tensor_scalar(s["var_eps"][:], s["mv"][:, :, 1], LN_EPS, None, ALU.add).then_inc(s["ln_step"], 1)


def norm_root(nc, pool, b, s):
    reach(pool, s["ln_step"], LN_STEPS * b + 2 * TI + 1)
    nc.gpsimd.tensor_tensor(s["rstd"][:], s["var_eps"][:], s["minus_half"][:], ALU.pow).then_inc(s["root_made"], 1)


def norm_apply(nc, dve, b, s):
    reach(dve, s["root_made"], b + 1)
    for i in range(TI):
        nc.vector.tensor_scalar(s["res"][:, i, :], s["res"][:, i, :], s["mv"][:, i, 0:1], s["rstd"][:, i:i + 1],
                                ALU.subtract, ALU.mult).then_inc(s["ln_step"], 1)


FF_COLS = {}
_at = 0
for _name, _kt, _cols in (("w1", DT, F), ("w2", DT, F), ("h1", FT, F), ("h2", FT, F), ("w3", FT, D)):
    FF_COLS[_name] = (_at, _kt, _cols)
    _at += _kt * _cols
FF_TOTAL = _at
PIECE = FT * T
PIECES = [(n, at + i, min(PIECE, kt * cols - i)) for n, (at, kt, cols) in FF_COLS.items()
          for i in range(0, kt * cols, PIECE)]


def feed_forward_phase(nc, a, x1, wf, out):
    with ExitStack() as ctx:
        def sb(name, shape, dt=F32):
            return ctx.enter_context(nc.sbuf_tensor("f_" + name, shape, dt))

        def sem(name):
            return ctx.enter_context(nc.semaphore("f_" + name))

        def bank(name):
            return ctx.enter_context(nc.psum_tensor("f_" + name, [P, 512], F32))
        RING = 4
        f_bank = [bank(f"layer_bank{i}") for i in range(RING)]
        turn_bank = [bank(f"turn_bank{i}") for i in range(DT)]
        out_bank = [bank(f"out_bank{i}") for i in range(2)]

        w_all = sb("w_all", [P, FF_TOTAL], F32R)
        w = {n: w_all[:, at:at + kt * cols].rearrange("p (k m) -> p k m", k=kt) for n, (at, kt, cols) in FF_COLS.items()}
        scales = sb("scales", [P, 4, FT])
        s3 = sb("s3", [P, 2, D])
        ident = sb("ident", [P, P])
        ones = sb("ones", [P, 2])
        differ = sb("differ", [P, len(PIECES)])
        inexact = sb("inexact", [1, 2], I32)
        x_turn, x_res = sb("x_turn", [P, TI, D]), sb("x_res", [P, TI, D])
        xt_hi, xt_lo = sb("xt_hi", [P, DT, T], F32R), sb("xt_lo", [P, DT, T], F32R)
        ha_hi, ha_lo = sb("ha_hi", [P, FT, T], F32R), sb("ha_lo", [P, FT, T], F32R)
        hb_hi, hb_lo = sb("hb_hi", [P, FT, T], F32R), sb("hb_lo", [P, FT, T], F32R)
        silu = [sb(f"silu{i}", [P, T]) for i in range(2)]
        h_full = [sb(f"h_full{i}", [P, T]) for i in range(2)]
        res = sb("res", [P, TI, D])
        stats, mv = sb("stats", [P, TI, 6]), sb("mv", [P, TI, 2])
        var_eps, rstd, minus_half = sb("var_eps", [P, TI]), sb("rstd", [P, TI]), sb("minus_half", [P, TI])

        ones_made = sem("ones_made")
        piece_hi, piece_compared = sem("piece_hi"), sem("piece_compared")
        differ_summed, total_made, inexact_made = sem("differ_summed"), sem("total_made"), sem("inexact_made")
        consts_in = sem("consts_in")
        w_in = {n: sem(f"{n}_in") for n in FF_COLS}
        turn_in, res_in = sem("turn_in"), sem("res_in")
        turned = sem("turned")
        turned_hi, turned_lo = sem("turned_hi"), sem("turned_lo")
        LAYER_TILES = 4 * FT
        f_ready = sem("f_ready")
        silu_done, gate_done = sem("silu_done"), sem("gate_done")
        gelu_done = sem("gelu_done")
        h_hi_made, h_split = sem("h_hi_made"), sem("h_split")
        y_ready, y_scaled = sem("y_ready"), sem("y_scaled")
        res_made = sem("res_made")
        ln_step, root_made, minus_half_made = sem("ln_step"), sem("root_made"), sem("minus_half_made")
        stored = sem("stored")
        sp_passed, dve_passed = sem("sp_passed"), sem("dve_passed")

        norm = dict(passed=dve_passed, ln_step=ln_step, root_made=root_made, res=res, stats=stats, mv=mv, var_eps=var_eps,
                          minus_half=minus_half, rstd=rstd)
        block = ctx.enter_context(nc.Block())

        @block.sync
        def _(sp):
            sp.dma_start(ident[:], a["ident"]).then_inc(consts_in, 16)
            sp.dma_start(scales[:], a["scales"]).then_inc(consts_in, 16)
            for i in range(2):
                sp.dma_start(s3[:, i, :], a["s3"].partition_broadcast(P)).then_inc(consts_in, 16)
            sp.dma_start(x_turn[:], x1[0]).then_inc(turn_in, 16)
            for n, (at, kt, cols) in FF_COLS.items():
                sp.dma_start(w_all[:, at:at + kt * cols].bitcast(F32), wf[:, at:at + kt * cols]).then_inc(w_in[n], 16)

            def load(c):
                reach_alone(sp, turned, 2 * c + 2, sp_passed)
                sp.dma_start(x_turn[:], x1[(c + 1) % BATCH]).then_inc(turn_in, 16)
                reach_alone(sp, res_made, 2 * c, sp_passed)
                sp.dma_start(x_res[:], x1[c]).then_inc(res_in, 16)

            def store(c):
                reach_alone(sp, ln_step, LN_STEPS * c + LN_STEPS, sp_passed)
                sp.dma_start(out[c].rearrange("(i p) d -> p i d", p=P), res[:]).then_inc(stored, 16)

            load(0)
            with sp.Fori(1, BATCH) as c:
                load(c)
                store(c - 1)
            store(BATCH - 1)
            sp.wait_ge(stored, 16 * BATCH)

        @block.gpsimd
        def _(pool):
            nc.gpsimd.memset(minus_half[:], -0.5).then_inc(minus_half_made, 1)
            pool.wait_ge(minus_half_made, 1)
            with pool.Fori(0, BATCH) as c:
                norm_root(nc, pool, c, norm)

        @block.scalar
        def _(act):
            for n, (name, at, cols) in enumerate(PIECES):
                act.wait_ge(w_in[name], 16)
                if n >= 2:
                    act.wait_ge(piece_compared, n - 1)
                hi = (ha_hi, hb_hi)[n % 2][:].rearrange("p k t -> p (k t)")
                nc.scalar.copy(hi[:, 0:cols], w_all[:, at:at + cols].bitcast(F32)).then_inc(piece_hi, 1)
            act.wait_ge(consts_in, 64)

            def turn_hi(c, ct):
                act.wait_ge(turned, 2 * c + ct + 1)
                nc.scalar.copy(xt_hi[:, ct, :], turn_bank[ct][:]).then_inc(turned_hi, 1)

            def gated(c, m):
                act.wait_ge(f_ready, LAYER_TILES * c + 2 * m + 1)
                if m >= 2:
                    act.wait_ge(gate_done, FT * c + m - 1)
                nc.scalar.activation(silu[m % 2][:], f_bank[2 * m % RING][:], ACT.Silu,
                                     scale=scales[:, 0, m:m + 1]).then_inc(silu_done, 1)

            def gate_hi(c, m):
                act.wait_ge(gate_done, FT * c + m + 1)
                nc.scalar.copy(ha_hi[:, m, :], h_full[m % 2][:]).then_inc(h_hi_made, 1)

            def gelu(c, layer, m):
                n = FT * layer + m
                act.wait_ge(f_ready, LAYER_TILES * c + FT + n + 1)
                act.wait_ge(h_split, 3 * FT * c + n - 1)
                nc.scalar.activation(h_full[m % 2][:], f_bank[m % RING][:], ACT.Gelu,
                                     scale=scales[:, 1 + layer, m:m + 1]).then_inc(gelu_done, 1)

            for ct in range(DT):
                turn_hi(0, ct)
            with act.Fori(0, BATCH) as c:
                for m in range(FT):
                    gated(c, m)
                    if m > 0:
                        gate_hi(c, m - 1)
                gate_hi(c, FT - 1)
                for layer in (1, 2):
                    for m in range(FT):
                        gelu(c, layer, m)
                        if layer == 2 and m in (3, 4):
                            turn_hi(c + 1, m - 3)

        @block.vector
        def _(dve):
            nc.vector.memset(ones[:], 1.0).then_inc(ones_made, 1)
            for n, (name, at, cols) in enumerate(PIECES):
                dve.wait_ge(piece_hi, n + 1)
                if n >= 2:
                    dve.wait_ge(piece_compared, n - 1)
                hi, flags = (b[n % 2][:].rearrange("p k t -> p (k t)")[:, 0:cols] for b in ((ha_hi, hb_hi), (ha_lo, hb_lo)))
                nc.vector.scalar_tensor_tensor(out=flags, in0=w_all[:, at:at + cols].bitcast(F32), scalar=1.0, in1=hi.bitcast(F32),
                                               op0=ALU.mult, op1=ALU.not_equal,
                                               accum_out=differ[:, n:n + 1]).then_inc(piece_compared, 1)
            dve.wait_ge(differ_summed, 1)
            nc.vector.tensor_reduce(ones[0:1, 0:1], out_bank[0][0:1, 0:len(PIECES)], AX.X, ALU.add).then_inc(total_made, 1)
            dve.wait_ge(total_made, 1)
            nc.vector.tensor_copy(inexact[0:1, 0:1], ones[0:1, 0:1]).then_inc(inexact_made, 1)
            dve.wait_ge(consts_in, 64)

            def turn_lo(c, ct):
                dve.wait_ge(turned_hi, 2 * c + ct + 1)
                nc.vector.tensor_tensor(xt_lo[:, ct, :], turn_bank[ct][:], xt_hi[:, ct, :].bitcast(F32),
                                        ALU.subtract).then_inc(turned_lo, 1)

            def lo(c, n, hi_buf, lo_buf):
                m = n % FT
                dve.wait_ge(h_hi_made, 3 * FT * c + n + 1)
                nc.vector.tensor_tensor(lo_buf[:, m, :], h_full[m % 2][:], hi_buf[:, m, :].bitcast(F32),
                                        ALU.subtract).then_inc(h_split, 1)

            def gate(c, m):
                dve.wait_ge(f_ready, LAYER_TILES * c + 2 * m + 2)
                dve.wait_ge(silu_done, FT * c + m + 1)
                if m >= 2:
                    dve.wait_ge(h_split, 3 * FT * c + m - 1)
                nc.vector.scalar_tensor_tensor(out=h_full[m % 2][:], in0=f_bank[(2 * m + 1) % RING][:],
                                               scalar=scales[:, 1, m:m + 1], in1=silu[m % 2][:],
                                               op0=ALU.mult, op1=ALU.mult).then_inc(gate_done, 1)

            def output(c, part):
                if part in (1, 2):
                    half = part - 1
                    two = slice(2 * half, 2 * half + 2)
                    reach(dve, stored, 16 * c)
                    dve.wait_ge(y_ready, 2 * c + half + 1)
                    nc.vector.tensor_tensor(res[:, two, :], out_bank[half][:].rearrange("p (i d) -> p i d", i=2), s3[:],
                                            ALU.mult).then_inc(y_scaled, 1)
                if part == 3:
                    dve.wait_ge(res_in, 16 * c + 16)
                    for half in range(2):
                        two = slice(2 * half, 2 * half + 2)
                        dve.wait_ge(y_scaled, 2 * c + half + 1)
                        nc.vector.tensor_tensor(res[:, two, :], res[:, two, :], x_res[:, two, :], ALU.add).then_inc(res_made, 1)
                if part == 4:
                    dve.wait_ge(res_made, 2 * c + 2)
                    norm_statistics(nc, dve, c, norm)
                if part == 6:
                    norm_apply(nc, dve, c, norm)

            def chunk(c, before=None):
                for m in range(FT):
                    gate(c, m)
                    if m > 0:
                        lo(c, m - 1, ha_hi, ha_lo)
                    if before is not None:
                        output(before, m)
                lo(c, FT - 1, ha_hi, ha_lo)
                for layer in (1, 2):
                    hi_buf, lo_buf = ((hb_hi, hb_lo), (ha_hi, ha_lo))[layer - 1]
                    for m in range(FT):
                        dve.wait_ge(gelu_done, 2 * FT * c + FT * (layer - 1) + m + 1)
                        nc.vector.tensor_copy(hi_buf[:, m, :], h_full[m % 2][:]).then_inc(h_hi_made, 1)
                        lo(c, FT * layer + m, hi_buf, lo_buf)
                        if layer == 2 and m in (3, 4):
                            turn_lo(c + 1, m - 3)

            for ct in range(DT):
                turn_lo(0, ct)
            chunk(0)
            with dve.Fori(1, BATCH) as c:
                chunk(c, c - 1)
            for part in range(FT):
                output(BATCH - 1, part)

        @block.tensor
        def _(pe):
            pe.wait_ge(consts_in, 64)
            pe.wait_ge(ones_made, 1)

            def turn(c):
                pe.wait_ge(turn_in, 16 * c + 16)
                for ct in range(DT):
                    for i in range(TI):
                        mm = nc.tensor.transpose(turn_bank[ct][:, P * i:P * i + P], x_turn[:, i, P * ct:P * ct + P], ident[:])
                    mm.then_inc(turned, 1)

            def layers(dt):
                def both(out, weight, hi, lo, first, last, weight_left=True):
                    for n, half in enumerate((hi, lo)):
                        left, right = (weight, half) if weight_left else (half, weight)
                        mm = nc.tensor.matmul(out, left.bitcast(dt), right.bitcast(dt),
                                              start=first and n == 0, stop=last and n == 1)
                    return mm

                with pe.Fori(0, BATCH) as c:
                    pe.wait_ge(turned_lo, 2 * c + 2)
                    for m in range(FT):
                        for n, name in enumerate(("w1", "w2")):
                            g = 2 * m + n
                            if m >= 2:
                                pe.wait_ge((silu_done, gate_done)[n], FT * c + m - 1)
                            for kt in range(DT):
                                mm = both(f_bank[g % RING][:], w[name][:, kt, P * m:P * m + P],
                                          xt_hi[:, kt, :], xt_lo[:, kt, :], kt == 0, kt == DT - 1)
                            mm.then_inc(f_ready, 1)
                    for layer, (name, hi, lo) in enumerate((("h1", ha_hi, ha_lo), ("h2", hb_hi, hb_lo))):
                        for m in range(FT):
                            n = FT * layer + m
                            if n < RING:
                                pe.wait_ge(gate_done, FT * c + FT - 1 + n // 2)
                            else:
                                pe.wait_ge(gelu_done, 2 * FT * c + n - RING + 1)
                            for kt in range(FT):
                                if m == 0:
                                    pe.wait_ge(h_split, 3 * FT * c + FT * layer + kt + 1)
                                mm = both(f_bank[m % RING][:], w[name][:, kt, P * m:P * m + P],
                                          hi[:, kt, :], lo[:, kt, :], kt == 0, kt == FT - 1)
                            mm.then_inc(f_ready, 1)
                            if layer == 1 and m == 3:
                                pe.wait_ge(turned_lo, 2 * c + 2)
                                turn(c + 1)
                    for i in range(TI):
                        tok = slice(P * i, P * i + P)
                        for kt in range(FT):
                            if i == 0:
                                pe.wait_ge(h_split, 3 * FT * c + 2 * FT + kt + 1)
                            mm = both(out_bank[i // 2][:, D * (i % 2):D * (i % 2) + D], w["w3"][:, kt, :],
                                      ha_hi[:, kt, tok], ha_lo[:, kt, tok], kt == 0, kt == FT - 1, weight_left=False)
                        if i % 2:
                            mm.then_inc(y_ready, 1)

            turn(0)
            pe.wait_ge(piece_compared, len(PIECES))
            nc.tensor.matmul(out_bank[0][0:1, 0:len(PIECES)], ones[:, 1:2], differ[:], start=True,
                             stop=True).then_inc(differ_summed, 1)
            pe.wait_ge(inexact_made, 1)
            bits = pe.value_load(inexact[0:1, 0:1], min_val=0)
            with pe.If(bits == 0):
                layers(F32R)
            with pe.Else():
                layers(F32)


def build(nc, a, out):
    x1 = nc.dram_tensor("x1", [BATCH, P, TI, D], F32, kind="Internal").ap()
    wf = nc.dram_tensor("wf_copy", [P, FF_TOTAL], F32, kind="Internal").ap()
    with nc.semaphore("wf_copied") as wf_copied, nc.Block() as block:
        @block.sync
        def _(sp):
            sp.dma_start(wf, a["wf"]).then_inc(wf_copied, 16)
            sp.wait_ge(wf_copied, 16)
    attention_phase(nc, a, x1)
    feed_forward_phase(nc, a, x1, wf, out)


def kernel(L0_attn_x, L0_attn_w_qkv, L0_attn_w_ky, L0_attn_w_proj, L0_ffn_w1_w, L0_ffn_w1_s, L0_ffn_w2_w,
           L0_ffn_w2_s, L0_ffn_h1_w, L0_ffn_h1_s, L0_ffn_h2_w, L0_ffn_h2_s, L0_ffn_w3_w, L0_ffn_w3_s):
    from concourse import bacc
    from concourse.bass_utils import run_bass_kernel_spmd

    def tiles(w):
        return w.T.reshape(-1, P, w.shape[0]).transpose(1, 0, 2)

    heads = np.arange(D).reshape(2, PAIRS, 2, HD)
    order = heads.transpose(0, 2, 3, 1).reshape(-1)
    wq, wk, wv = (L0_attn_w_qkv[D * i:D * i + D] for i in range(3))
    w4 = np.stack([tiles(w) for w in (wq[order], L0_attn_w_ky[order], wk[order], wv)], axis=2)

    x = L0_attn_x
    arrays = {
        "xt": x.transpose(0, 2, 1).reshape(BATCH, DT, P, T).transpose(0, 2, 1, 3),
        "xn": x.reshape(BATCH, TI, P, D).transpose(0, 2, 1, 3),
        "w4": w4,
        "wp": tiles(L0_attn_w_proj),
        "ident": np.eye(P, dtype=np.float32),
        "tri": np.stack([np.triu(np.ones((P, P), np.float32)), np.ones((P, P), np.float32)], axis=1),
        "count": np.arange(1, T + 1, dtype=np.float32).reshape(TI, P).T,
        "wf": np.concatenate([tiles(w).reshape(P, -1) for w in
                              (L0_ffn_w1_w, L0_ffn_w2_w, L0_ffn_h1_w, L0_ffn_h2_w, L0_ffn_w3_w)], axis=1),
        "scales": np.stack([s.reshape(FT, P).T for s in
                            (L0_ffn_w1_s, L0_ffn_w2_s, L0_ffn_h1_s, L0_ffn_h2_s)], axis=1),
        "s3": L0_ffn_w3_s,
    }
    arrays = {f"in_{n}": np.ascontiguousarray(v) for n, v in arrays.items()}
    nc = bacc.Bacc("TRN2", target_bir_lowering=False, num_devices=1)
    a = {n[3:]: nc.dram_tensor(n, v.shape, mybir.dt.from_np(v.dtype), kind="ExternalInput").ap() for n, v in arrays.items()}
    out = nc.dram_tensor("out", (BATCH, T, D), F32, kind="ExternalOutput").ap()
    build(nc, a, out)
    return run_bass_kernel_spmd(nc, [arrays], core_ids=[0]).results[0]["out"]
```

```python
import math
from contextlib import ExitStack

import numpy as np

import concourse.bass as bass
from concourse import mybir

F32 = mybir.dt.float32
F32R = mybir.dt.float32r
I32 = mybir.dt.int32
ALU = mybir.AluOpType
ACT = mybir.ActivationFunctionType
AX = mybir.AxisListType

P = 128
BATCH, T, D = 8, 512, 256
H, HD = 16, 16
F = 1024
TI = T // P
DT = D // P
FT = F // P
HU = H // 2
PAIRS = HU // 2
UNITS = 2 * BATCH
COPIES = 4
SW = 32
ONE, EXP = HD, HD + 1
USED = HD + 2
STEPS = PAIRS
LAG = 2
KEY_TILES = ((0, 3), (1, 2))
EPS = 1e-6
LN_EPS = 1e-5
CLIP = 15.0
FF_COLS = {}
_at = 0
for _name, _kt, _cols in (("w1", DT, F), ("w2", DT, F), ("h1", FT, F), ("h2", FT, F), ("w3", FT, D)):
    FF_COLS[_name] = (_at, _kt, _cols)
    _at += _kt * _cols
FF_TOTAL = _at
PIECE = 512
PIECES = FF_TOTAL // PIECE
CHUNKS = 3
W_AT = (0, 512, 1024, 896)
W_COLS = 1280
CHUNK_COLS = ((0, 512), (512, 512), (1024, 256))
STACK_DMAS = 2 * COPIES
LN_STEPS = 3 * TI + 1
ATT_STEPS = 4


class Unit:

    def __init__(self, batch, half):
        self.batch, self.half = batch, half
        self.index = 2 * batch + half

    def shift(self, n):
        half = self.half + n
        return Unit(self.batch + half // 2, half % 2)


FIRST_W = STEPS + LAG
FIRST_CHECK = 3


def reach(engine, sem, value):
    if isinstance(value, int) and value <= 0:
        return
    engine.wait_ge(sem, value)


def at_most(value, limit):
    return min(value, limit) if isinstance(value, int) else value


def reach_alone(engine, sem, value, passed):
    reach(engine, sem, value)
    engine.sem_inc(passed, 1)




def attention_phase(nc, a, x1, wf, differ_sum):
    with ExitStack() as ctx:
        def sb(name, shape, dt=F32):
            return ctx.enter_context(nc.sbuf_tensor(name, shape, dt))

        def sem(name):
            return ctx.enter_context(nc.semaphore(name))

        def bank(name):
            return ctx.enter_context(nc.psum_tensor(name, [P, 512], F32))
        y_bank = [bank("y_bank0"), bank("y_bank1")]
        w_bank = [bank("w_bank0"), bank("w_bank1"), bank("w_bank2")]
        acc = bank("acc_bank")
        flip = bank("flip_bank")
        misc = bank("misc_bank")

        w_hi = sb("w_hi", [P, DT, 4, D], F32R)
        w_lo = sb("w_lo", [P, DT, 4, D], F32R)
        wp_hi = sb("wp_hi", [P, DT, D], F32R)
        wp_lo = sb("wp_lo", [P, DT, D], F32R)
        ident = sb("ident", [P, P])
        tri = sb("tri", [P, 2, P])
        count = sb("count", [P, TI])
        sum_exp = sb("sum_exp", [P, SW])
        xt_raw = sb("xt_raw", [P, DT, T])
        xt_hi = sb("xt_hi", [P, DT, T], F32R)
        xt_lo = sb("xt_lo", [P, DT, T], F32R)
        x_nat = sb("x_nat", [P, TI, D])
        q_full = [sb(f"q_full{t}", [P, T]) for t in range(2)]
        q_hi, q_lo = sb("q_hi", [P, T], F32R), sb("q_lo", [P, T], F32R)
        ky_hi, ky_lo = sb("ky_hi", [P, T], F32R), sb("ky_lo", [P, T], F32R)
        k_hi, k_lo = sb("k_hi", [P, T], F32R), sb("k_lo", [P, T], F32R)
        qc_hi, qc_lo = sb("qc_hi", [P, T], F32R), sb("qc_lo", [P, T], F32R)
        q_stack = [sb(f"q_stack{t}", [P, PAIRS, T], F32R) for t in range(2)]
        ky_stack = [sb(f"ky_stack{t}", [P, PAIRS, T], F32R) for t in range(2)]
        k_stack = [sb(f"k_stack{t}", [P, PAIRS, T], F32R) for t in range(2)]
        qc_stack = [sb(f"qc_stack{t}", [P, PAIRS, T], F32R) for t in range(2)]
        v_stage = sb("v_stage", [P, TI, HU, HD])
        v_aug = [sb(f"v_aug{t}", [P, TI, HU, SW]) for t in range(2)]
        RING = 4
        e_ring, w_ring = sb("e_ring", [P, RING, W_COLS]), sb("w_ring", [P, RING, W_COLS])
        e_buf, w_buf = ([ring[:, i, :] for i in range(RING)] for ring in (e_ring, w_ring))
        w_raw = e_ring[:].rearrange("p r c -> p (r c)")[:, 0:DT * 4 * D].rearrange("p (k n c) -> p k n c", k=DT, n=4)
        wp_raw = w_buf[0][:, 0:DT * D].rearrange("p (k c) -> p k c", k=DT)
        acc_copy = sb("acc_copy", [P, T])
        acc_turned = sb("acc_turned", [P, TI, 2, 2, USED])
        agg = [sb(f"agg{t}", [P, TI, HU]) for t in range(2)]
        agg_eps = sb("agg_eps", [P, TI, 2 * HU])
        c_cols = sb("c_cols", [P, TI, 2 * HU])
        c_spread = sb("c_spread", [P, TI, 2, HD, PAIRS])
        att_raw = sb("att_raw", [P, TI, H, HD + 1])
        base = sb("base", [P, TI, H])
        v_sum = sb("v_sum", [P, TI, H, HD])
        base_v = sb("base_v", [P, TI, H, HD])
        att = base_v[:].rearrange("p i h d -> p i (h d)")
        base_sum = sb("base_sum", [P, TI, H])
        att_den = sb("att_den", [P, TI * H])
        att_inv = sb("att_inv", [P, TI * H])
        att_hi, att_lo = sb("att_hi", [P, DT, T], F32R), sb("att_lo", [P, DT, T], F32R)
        piece, piece_hi = sb("piece", [P, PIECE]), sb("piece_hi", [P, PIECE], F32R)
        differ = sb("differ", [P, STEPS])
        res = sb("res", [P, TI, D])
        stats, mv = sb("stats", [P, TI, 6]), sb("mv", [P, TI, 2])
        var_eps, rstd, minus_half = sb("var_eps", [P, TI]), sb("rstd", [P, TI]), sb("minus_half", [P, TI])

        acc_zeroed = sem("acc_zeroed")
        made_once = sem("made_once")
        consts_in = sem("consts_in")
        kind_in = [sem(f"kind_in{n}") for n in range(4)]
        weights_hi, weights_lo = sem("weights_hi"), sem("weights_lo")
        xt_in = sem("xt_in")
        xn_in = sem("xn_in")
        xt_split = sem("xt_split")
        xt_hi_made = sem("xt_hi_made")
        k_ready, v_ready = sem("k_ready"), sem("v_ready")
        q_ready, ky_ready = sem("q_ready"), sem("ky_ready")
        k_hi_made, k_lo_made = sem("k_hi_made"), sem("k_lo_made")
        q_hi_made, q_lo_made = sem("q_hi_made"), sem("q_lo_made")
        ky_hi_made, ky_lo_made = sem("ky_hi_made"), sem("ky_lo_made")
        v_staged, v_spread = sem("v_staged"), sem("v_spread")
        q_stacked = [sem(f"q_stacked{t}") for t in range(2)]
        ky_stacked = [sem(f"ky_stacked{t}") for t in range(2)]
        k_stacked = [sem(f"k_stacked{t}") for t in range(2)]
        qc_stacked = [sem(f"qc_stacked{t}") for t in range(2)]
        y_scores = sem("y_scores")
        exp_done = sem("exp_done")
        e_clipped = sem("e_clipped")
        e_masked = sem("e_masked")
        w_scores = sem("w_scores")
        abs_done = sem("abs_done")
        ln_done = sem("ln_done")
        w_masked = sem("w_masked")
        acc_done = sem("acc_done")
        acc_copied = sem("acc_copied")
        acc_flipped = sem("acc_flipped")
        acc_kept = sem("acc_kept")
        agg_added, att_added = sem("agg_added"), sem("att_added")
        cols_step = sem("cols_step")
        spread_ready = sem("spread_ready")
        qc_made = sem("qc_made")
        qc_hi_made, qc_lo_made = sem("qc_hi_made"), sem("qc_lo_made")
        base_made = sem("base_made")
        v_sum_ready, v_sum_copied = sem("v_sum_ready"), sem("v_sum_copied")
        base_step = sem("base_step")
        att_step = sem("att_step")
        turned = sem("turned")
        turned_hi, turned_lo = sem("turned_hi"), sem("turned_lo")
        proj_ready = sem("proj_ready")
        res_made = sem("res_made")
        ln_step = sem("ln_step")
        root_made = sem("root_made")
        x1_stored = sem("x1_stored")
        piece_in, piece_split, piece_compared = sem("piece_in"), sem("piece_split"), sem("piece_compared")
        differ_added, wf_copied = sem("differ_added"), sem("wf_copied")
        pool_passed, sp_passed, dve_passed = sem("pool_passed"), sem("sp_passed"), sem("dve_passed")

        norm_tiles = dict(passed=dve_passed, ln_step=ln_step, root_made=root_made, res=res, stats=stats, mv=mv, var_eps=var_eps,
                          minus_half=minus_half, rstd=rstd)
        rows = [slice(64 * par, 64 * par + 64) for par in range(2)]
        block = ctx.enter_context(nc.Block())

        def tiles_of(c):
            return (((0, 0),), ((0, 1), (384, 3)), ((0, 2),))[c]

        def weights_of(k, s):
            return (k.shift(-2), s + LAG) if s < LAG else (k.shift(-1), s - LAG)

        def step_of(u, m):
            return STEPS * (u.index + 1) + LAG + m

        ALL, NONE = (0, 1, 2, 3), ()

        def run(slot, fori):
            slot(Unit(0, 0), w=NONE, before=(False, False))
            slot(Unit(0, 1), w=(2, 3), before=(True, False), x=1)
            slot(Unit(1, 0))
            slot(Unit(1, 1), x=2, divide=0, check=True)
            with fori(2, BATCH - 1) as j:
                slot(Unit(j, 0), out=j - 2, first_in_loop=True, check=True)
                slot(Unit(j, 1), x=j + 1, divide=j - 1, norm=j - 2, check=True)
            slot(Unit(BATCH - 1, 0), out=BATCH - 3, first_in_loop=True)
            slot(Unit(BATCH - 1, 1), project=False, divide=BATCH - 2, norm=BATCH - 3)
            slot(Unit(BATCH, 0), y=False, project=False, out=BATCH - 2)
            slot(Unit(BATCH, 1), y=False, project=False, w=(0, 1), before=(False, True), divide=BATCH - 1, norm=BATCH - 2)
            slot(Unit(BATCH + 1, 0), y=False, project=False, w=NONE, before=(False, False), out=BATCH - 1)
            slot(Unit(BATCH + 1, 1), y=False, project=False, w=NONE, before=(False, False), norm=BATCH - 1)

        def sums_of(s, y, w, before):
            return before if s == 0 else (y, s - 1 in w)

        @block.sync
        def _(sp):
            sp.dma_start(xt_raw[:], a["xt"][0]).then_inc(xt_in, 16)
            for n in range(4):
                sp.dma_start(w_raw[:, :, n, :], a["w4"][:, :, n, :]).then_inc(kind_in[n], 16)
            sp.dma_start(ident[:], a["ident"]).then_inc(consts_in, 16)
            sp.dma_start(wp_raw, a["wp"]).then_inc(consts_in, 16)
            sp.dma_start(tri[:], a["tri"]).then_inc(consts_in, 16)
            sp.dma_start(count[:], a["count"]).then_inc(consts_in, 16)

            def stack(dst, hi, lo, hi_made, lo_made, copies, used, u, sem):
                reach_alone(sp, hi_made, u.index + 1, sp_passed)
                reach(sp, used, 24 * (u.index - 1))
                for half, src in enumerate((hi, lo)):
                    if half == 1:
                        reach(sp, lo_made, u.index + 1)
                    for r in (r for r in range(COPIES) if copies[r] == half):
                        for par in range(2):
                            to = dst[u.half][64 * par + HD * r:64 * par + HD * r + HD, :, :]
                            sp.dma_start(to.bitcast(F32), src[64 * par:64 * par + 64, :].bitcast(F32)).then_inc(sem[u.half], 16)
            LEFT, RIGHT = (0, 0, 1, 1), (0, 1, 0, 1)

            def stack_q(u):
                stack(q_stack, q_hi, q_lo, q_hi_made, q_lo_made, RIGHT, y_scores, u, q_stacked)

            def stack_ky(u):
                stack(ky_stack, ky_hi, ky_lo, ky_hi_made, ky_lo_made, LEFT, y_scores, u, ky_stacked)

            def stack_qc(v):
                stack(qc_stack, qc_hi, qc_lo, qc_hi_made, qc_lo_made, RIGHT, w_scores, v, qc_stacked)

            def stack_k(u):
                stack(k_stack, k_hi, k_lo, k_hi_made, k_lo_made, LEFT, w_scores, u, k_stacked)

            def load_piece(k, s):
                n = STEPS * (k.index - FIRST_CHECK) + s
                reach_alone(sp, piece_compared, n, sp_passed)
                sp.dma_start(piece[:], a["wf"][n]).then_inc(piece_in, 16)

            def slot(k, y=True, project=True, w=ALL, x=None, divide=None, out=None, norm=None, check=False, **_):
                if x is not None:
                    reach_alone(sp, xt_split, x, sp_passed)
                    sp.dma_start(xt_raw[:], a["xt"][x]).then_inc(xt_in, 16)
                if check:
                    load_piece(k, 0)
                if out is not None:
                    reach_alone(sp, res_made, 2 * out, sp_passed)
                    sp.dma_start(x_nat[:], a["xn"][out]).then_inc(xn_in, 16)
                if project:
                    stack_ky(k.shift(1))
                if check:
                    load_piece(k, 1)
                if 2 in w:
                    stack_qc(k.shift(-1))
                if y:
                    stack_k(k)
                if check:
                    load_piece(k, 2)
                if project:
                    stack_q(k.shift(1))
                if norm is not None:
                    reach_alone(sp, ln_step, LN_STEPS * (norm + 1), sp_passed)
                    sp.dma_start(x1[norm], res[:]).then_inc(x1_stored, 16)
                if check:
                    f = k.index - FIRST_CHECK
                    sp.dma_start(wf[f], a["wf"].rearrange("(f s) p c -> f s p c", s=STEPS)[f]).then_inc(wf_copied, 16)
                    load_piece(k, 3)

            stack_q(Unit(0, 0))
            stack_ky(Unit(0, 0))
            run(slot, sp.Fori)
            sp.wait_ge(x1_stored, 16 * BATCH)
            sp.wait_ge(wf_copied, 16 * PIECES // STEPS)

        @block.gpsimd
        def _(pool):
            for t in range(2):
                nc.gpsimd.memset(v_aug[t][:, :, :, HD:SW], 0.0)
            nc.gpsimd.memset(minus_half[:], -0.5)
            nc.gpsimd.memset(sum_exp[:], 0.0).then_inc(made_once, 1)
            pool.wait_ge(made_once, 1)
            for t in range(2):
                nc.gpsimd.memset(v_aug[t][:, :, :, ONE:ONE + 1], 1.0)
            nc.gpsimd.memset(sum_exp[:, EXP:EXP + 1], 1.0).then_inc(made_once, 1)

            def mask(buf, done):
                for blocks in (buf[:, 0:1024].rearrange("p (b c) -> p b c", b=2)[:, :, 0:P],
                               buf[:, 896:1152].rearrange("p (b c) -> p b c", b=2)):
                    nc.gpsimd.affine_select(out=blocks, in_=blocks, compare_op=ALU.is_ge, fill=0.0, base=0,
                                            pattern=[[0, 2], [1, P]], channel_multiplier=-1).then_inc(done, 1)

            def mask_e(k, n):
                reach_alone(pool, e_clipped, HU * k.index + n + 1, pool_passed)
                mask(e_buf[n % RING], e_masked)

            def mask_w(u, n):
                reach_alone(pool, ln_done, HU * u.index + n + 1, pool_passed)
                mask(w_buf[n % RING], w_masked)

            def spread_values(u):
                reach(pool, v_staged, u.index + 1)
                reach_alone(pool, acc_done, step_of(u.shift(-2), PAIRS - 1) + 1, pool_passed)
                nc.gpsimd.tensor_copy(v_aug[u.half][:, :, :, 0:HD], v_stage[:]).then_inc(v_spread, 1)

            def base_times(b):
                reach(pool, v_sum_copied, 2 * (b + 1))
                reach(pool, base_made, 2 * (b + 1))
                reach(pool, turned, 2 * b)
                nc.gpsimd.tensor_tensor(base_v[:].rearrange("p i h d -> p (i h) d"), v_sum[:].rearrange("p i h d -> p (i h) d"),
                                        base[:].rearrange("p i h -> p (i h)").unsqueeze(2).to_broadcast([P, TI * H, HD]),
                                        ALU.mult).then_inc(base_step, 1)
                nc.gpsimd.tensor_tensor(base_sum[:], base[:], count[:].unsqueeze(2).to_broadcast([P, TI, H]),
                                        ALU.mult).then_inc(base_step, 1)

            def keep_sums(k, s, y, w):
                reach(pool, acc_kept, STEPS * k.index + s + 1)
                if y:
                    nc.gpsimd.tensor_tensor(agg[k.half][:, :, 2 * s:2 * s + 2], acc_turned[:, :, :, 0, EXP],
                                            acc_turned[:, :, :, 1, EXP], ALU.add).then_inc(agg_added, 1)
                if w:
                    u, m = weights_of(k, s)
                    if m == 0 and u.half == 0:
                        reach(pool, att_step, ATT_STEPS * (u.batch - 1) + 2)
                    h = HU * u.half + 2 * m
                    nc.gpsimd.tensor_tensor(att_raw[:, :, h:h + 2, :], acc_turned[:, :, :, 0, 0:HD + 1],
                                            acc_turned[:, :, :, 1, 0:HD + 1], ALU.add).then_inc(att_added, 1)

            def slot(k, y=True, w=ALL, before=(True, True), divide=None, norm=None, **_):
                for s in range(STEPS):
                    sums = sums_of(s, y, w, before)
                    summed = (k, s - 1) if s else (k.shift(-1), STEPS - 1)
                    for par in range(2):
                        if y:
                            mask_e(k, 2 * s + par)
                        if par == 0 and sums[1]:
                            u, m = weights_of(*summed)
                            mask_w(u, 2 * m + 1)
                        if par == 1 and s in w:
                            u, m = weights_of(k, s)
                            mask_w(u, 2 * m)
                        if par == 0 and s == 3 and y:
                            spread_values(k)
                        if par == 0 and s == 0 and divide is not None:
                            base_times(divide)
                        if par == 0 and s == 0 and norm is not None:
                            norm_root(nc, pool, norm, norm_tiles)
                    if any(sums):
                        keep_sums(*summed, *sums)
            run(slot, pool.Fori)

        @block.scalar
        def _(act):
            nc.scalar.preload_act_table_set("natural_log_exp_and_others")

            def weights_split(n):
                act.wait_ge(kind_in[n], 16)
                nc.scalar.copy(w_hi[:, :, n, :], w_raw[:, :, n, :]).then_inc(weights_hi, 1)

            def split_x(b):
                reach(act, xt_in, 16 * (b + 1))
                reach(act, v_ready, 2 * b)
                nc.scalar.copy(xt_hi[:], xt_raw[:]).then_inc(xt_hi_made, 1)

            def stack_free(stacked, u):
                reach(act, stacked[u.half], 16 * STACK_DMAS * (u.batch + 1))

            def q_split(u):
                reach(act, q_ready, u.index + 1)
                reach(act, qc_hi_made, u.index - 1)
                reach(act, qc_lo_made, u.index - 1)
                nc.scalar.mul(q_full[u.half][:], misc[:], HD ** -0.5)
                stack_free(q_stacked, u.shift(-1))
                nc.scalar.mul(q_hi[:], misc[:], HD ** -0.5).then_inc(q_hi_made, 1)

            def ky_split(u):
                reach(act, ky_ready, u.index + 1)
                stack_free(ky_stacked, u.shift(-1))
                nc.scalar.copy(ky_hi[:], misc[:]).then_inc(ky_hi_made, 1)

            def k_split(u):
                reach(act, k_ready, u.index + 1)
                stack_free(k_stacked, u.shift(-1))
                nc.scalar.copy(k_hi[:], misc[:]).then_inc(k_hi_made, 1)

            def v_copy(u):
                reach(act, v_ready, u.index + 1)
                reach(act, v_spread, u.index)
                nc.scalar.copy(v_stage[:].rearrange("p i h d -> p (i h d)"), misc[:]).then_inc(v_staged, 1)

            def exps(k, s, par):
                n = 2 * s + par
                reach(act, acc_done, STEPS * k.index + s - 1)
                for c, (at, cols) in enumerate(CHUNK_COLS):
                    reach(act, y_scores, 24 * k.index + 3 * n + c + 1)
                    nc.scalar.activation(e_buf[n % RING][:, at:at + cols], y_bank[(3 * n + c) % 2][:, 0:cols], ACT.Exp).then_inc(exp_done, 1)

            def logs(u, m, par):
                n = 2 * m + par
                reach(act, abs_done, 24 * u.index + 3 * n + 3)
                nc.scalar.activation(w_buf[n % RING], w_buf[n % RING], ACT.Ln, bias=1.0).then_inc(ln_done, 1)

            def qc_split(v):
                reach(act, qc_made, v.index + 1)
                stack_free(qc_stacked, v.shift(-1))
                nc.scalar.copy(qc_hi[:], q_full[v.half][:]).then_inc(qc_hi_made, 1)

            def base_make(v):
                reach(act, cols_step, 5 * v.index + 3)
                if v.half == 0:
                    reach(act, base_step, 2 * v.batch)
                nc.scalar.activation(base[:, :, HU * v.half:HU * v.half + HU], c_cols[:, :, HU:2 * HU], ACT.Ln,
                                     bias=1.0, scale=EPS).then_inc(base_made, 1)

            def v_sum_copy(v):
                reach(act, v_sum_ready, v.index + 1)
                if v.half == 0:
                    reach(act, base_step, 2 * v.batch)
                nc.scalar.copy(v_sum[:, :, HU * v.half:HU * v.half + HU, :],
                               misc[:].rearrange("p (i h d) -> p i h d", i=TI, h=HU)).then_inc(v_sum_copied, 1)

            def turn_hi(b, ct):
                reach(act, turned, 2 * b + ct + 1)
                nc.scalar.copy(att_hi[:, ct, :], misc[:]).then_inc(turned_hi, 1)

            def copy_sums(step):
                reach(act, acc_done, step + 1)
                reach(act, acc_flipped, step)
                nc.scalar.copy(acc_copy[:], acc[:]).then_inc(acc_copied, 1)

            def keep_flipped(step, agg_count, att_count):
                reach(act, acc_flipped, step + 1)
                reach(act, agg_added, agg_count)
                reach(act, att_added, att_count)
                nc.scalar.copy(acc_turned[:].rearrange("p i r g c -> p i (r g) c"),
                               flip[:].rearrange("p (i g c) -> p i g c", i=TI, c=SW)[:, :, :, 0:USED]).then_inc(acc_kept, 1)

            def piece_halve(k, s):
                n = STEPS * (k.index - FIRST_CHECK) + s
                reach(act, piece_in, 16 * n + 16)
                reach(act, piece_compared, n)
                nc.scalar.copy(piece_hi[:], piece[:]).then_inc(piece_split, 1)

            def slot(k, y=True, project=True, w=ALL, before=(True, True), x=None, out=None, check=False, **_):
                for s in range(STEPS):
                    step = STEPS * k.index + s
                    sums = sums_of(s, y, w, before)
                    summed = (k, s - 1) if s else (k.shift(-1), STEPS - 1)
                    if y:
                        exps(k, s, 0)
                    if s == 0 and out is not None:
                        turn_hi(out, 0)
                    if s == 2 and 2 in w:
                        v_sum_copy(k.shift(-1))
                    if sums[1]:
                        logs(*weights_of(*summed), 1)
                    if s == 0 and x is not None:
                        split_x(x)
                    if s == 0 and out is not None:
                        turn_hi(out, 1)
                    if s == 1 and 2 in w:
                        base_make(k.shift(-1))
                        qc_split(k.shift(-1))
                    if y:
                        exps(k, s, 1)
                    if s in w:
                        logs(*weights_of(k, s), 0)
                    if any(sums):
                        copy_sums(step - 1)
                    if check:
                        piece_halve(k, s)
                    if project:
                        (ky_split, q_split, k_split, v_copy)[s](k.shift(1))
                    if any(sums):
                        keep_flipped(step - 1, at_most(step - 1, UNITS * PAIRS), at_most(step - 1 - FIRST_W, UNITS * PAIRS))

            split_x(0)
            weights_split(0)
            weights_split(1)
            q_split(Unit(0, 0))
            weights_split(2)
            ky_split(Unit(0, 0))
            weights_split(3)
            k_split(Unit(0, 0))
            act.wait_ge(consts_in, 64)
            nc.scalar.copy(wp_hi[:], wp_raw).then_inc(weights_hi, 1)
            v_copy(Unit(0, 0))
            run(slot, act.Fori)

        @block.vector
        def _(dve):
            nc.vector.memset(acc[:, 0:P], 0.0).then_inc(acc_zeroed, 1)
            nc.vector.memset(differ_sum[:], 0.0).then_inc(differ_added, 1)

            def weights_split(n):
                dve.wait_ge(weights_hi, n + 1)
                nc.vector.tensor_tensor(w_lo[:, :, n, :], w_raw[:, :, n, :], w_hi[:, :, n, :].bitcast(F32),
                                        ALU.subtract).then_inc(weights_lo, 1)

            def split_x(b):
                reach(dve, xt_hi_made, b + 1)
                nc.vector.tensor_tensor(xt_lo[:], xt_raw[:], xt_hi[:].bitcast(F32), ALU.subtract).then_inc(xt_split, 1)

            def lo_of(lo, hi, made, count, then, scale=1.0):
                reach(dve, made, count)
                nc.vector.scalar_tensor_tensor(out=lo, in0=misc[:], scalar=scale, in1=hi.bitcast(F32),
                                               op0=ALU.mult, op1=ALU.subtract).then_inc(then, 1)

            def stack_free(stacked, u):
                reach(dve, stacked[u.half], 16 * STACK_DMAS * (u.batch + 1))

            def q_split(u):
                stack_free(q_stacked, u.shift(-1))
                lo_of(q_lo[:], q_hi[:], q_hi_made, u.index + 1, q_lo_made, HD ** -0.5)

            def ky_split(u):
                stack_free(ky_stacked, u.shift(-1))
                lo_of(ky_lo[:], ky_hi[:], ky_hi_made, u.index + 1, ky_lo_made)

            def k_split(u):
                stack_free(k_stacked, u.shift(-1))
                lo_of(k_lo[:], k_hi[:], k_hi_made, u.index + 1, k_lo_made)

            def clip(k, n):
                reach(dve, exp_done, 24 * k.index + 3 * n + 3)
                nc.vector.tensor_scalar(e_buf[n % RING], e_buf[n % RING], math.exp(CLIP), math.exp(-CLIP),
                                        ALU.min, ALU.max).then_inc(e_clipped, 1)

            def absolute(k, s, par):
                u, m = weights_of(k, s)
                n = 2 * m + par
                reach(dve, acc_done, STEPS * k.index + s - 1)
                for c, (at, cols) in enumerate(CHUNK_COLS):
                    reach(dve, w_scores, 24 * u.index + 3 * n + c + 1)
                    nc.vector.tensor_scalar(w_buf[n % RING][:, at:at + cols].bitcast(I32), w_bank[c][:, 0:cols].bitcast(I32),
                                            0x7FFFFFFF, None, ALU.bitwise_and).then_inc(abs_done, 1)

            def factors(v):
                start = 5 * v.index
                reach(dve, agg_added, PAIRS * (v.index + 1))
                reach(dve, base_made, v.index)
                reach(dve, spread_ready, v.index)
                nc.vector.tensor_scalar(agg_eps[:, :, HU:2 * HU], agg[v.half][:], EPS, EPS, ALU.add, ALU.add).then_inc(cols_step, 1)
                reach(dve, cols_step, start + 1)
                nc.vector.tensor_scalar(agg_eps[:, :, 0:HU], agg_eps[:, :, HU:2 * HU], EPS, None, ALU.add).then_inc(cols_step, 1)
                reach(dve, cols_step, start + 2)
                nc.vector.reciprocal(c_cols[:], agg_eps[:]).then_inc(cols_step, 1)
                reach(dve, cols_step, start + 3)
                for par in range(2):
                    c = c_cols[:, :, 0:HU].rearrange("p i (q r) -> p i q r", r=2)[:, :, :, par]
                    nc.vector.tensor_copy(c_spread[:, :, par, :, :],
                                          c.unsqueeze(2).to_broadcast([P, TI, HD, PAIRS])).then_inc(cols_step, 1)

            def scale_q(v):
                reach(dve, spread_ready, v.index + 1)
                nc.vector.tensor_tensor(q_full[v.half][:], misc[:], q_full[v.half][:], ALU.mult).then_inc(qc_made, 1)

            def qc_split(v):
                stack_free(qc_stacked, v.shift(-1))
                reach(dve, qc_hi_made, v.index + 1)
                reach(dve, qc_made, v.index + 1)
                nc.vector.tensor_tensor(qc_lo[:], q_full[v.half][:], qc_hi[:].bitcast(F32), ALU.subtract).then_inc(qc_lo_made, 1)

            def normalise(b):
                start = ATT_STEPS * b
                reach(dve, att_added, 2 * PAIRS * (b + 1))
                reach(dve, base_step, 2 * (b + 1))
                reach(dve, turned, 2 * b)
                raw = att_raw[:].rearrange("p i h c -> p (i h) c")
                sums = base_v[:].rearrange("p i h d -> p (i h) d")
                nc.vector.scalar_tensor_tensor(out=att_den[:], in0=raw[:, :, ONE], scalar=EPS,
                                               in1=base_sum[:].rearrange("p i h -> p (i h)"),
                                               op0=ALU.add, op1=ALU.add).then_inc(att_step, 1)
                nc.vector.tensor_tensor(sums, sums, raw[:, :, 0:HD], ALU.add).then_inc(att_step, 1)
                reach(dve, att_step, start + 2)
                nc.vector.reciprocal(att_inv[:], att_den[:]).then_inc(att_step, 1)
                reach(dve, att_step, start + 3)
                nc.vector.tensor_tensor(sums, sums,
                                        att_inv[:].unsqueeze(2).to_broadcast([P, TI * H, HD]), ALU.mult).then_inc(att_step, 1)

            def residual(b, half):
                reach(dve, xn_in, 16 * (b + 1))
                reach(dve, x1_stored, 16 * b)
                reach(dve, proj_ready, 2 * b + half + 1)
                two = slice(2 * half, 2 * half + 2)
                nc.vector.tensor_tensor(res[:, two, :], misc[:].rearrange("p (i d) -> p i d", i=2), x_nat[:, two, :],
                                        ALU.add).then_inc(res_made, 1)

            def turn_lo(b, ct):
                lo_of(att_lo[:, ct, :], att_hi[:, ct, :], turned_hi, 2 * b + ct + 1, turned_lo)

            def compare_piece(k, s):
                f = k.index - FIRST_CHECK
                reach(dve, piece_split, STEPS * f + s + 1)
                reach(dve, differ_added, f + 1)
                nc.vector.scalar_tensor_tensor(out=piece_hi[:], in0=piece[:], scalar=1.0, in1=piece_hi[:].bitcast(F32),
                                               op0=ALU.mult, op1=ALU.not_equal,
                                               accum_out=differ[:, s:s + 1]).then_inc(piece_compared, 1)
                if s == STEPS - 1:
                    reach(dve, piece_compared, STEPS * (f + 1))
                    nc.vector.tensor_tensor(differ_sum[:], differ_sum[:], differ[:], ALU.add).then_inc(differ_added, 1)

            def slot(k, y=True, project=True, w=ALL, x=None, divide=None, out=None, norm=None, check=False, **_):
                for s in range(STEPS):
                    if s == 1 and 2 in w:
                        factors(k.shift(-1))
                    if y:
                        clip(k, 2 * s)
                    if s == 0 and out is not None:
                        turn_lo(out, 0)
                    if s == 1 and 2 in w:
                        scale_q(k.shift(-1))
                    if s in w:
                        absolute(k, s, 0)
                    if s == 0 and out is not None:
                        turn_lo(out, 1)
                    if s == 0 and x is not None:
                        split_x(x)
                    if s == 1 and 2 in w:
                        qc_split(k.shift(-1))
                    if s in (2, 3) and out is not None:
                        residual(out, s - 2)
                    if s == 3 and divide is not None:
                        normalise(divide)
                    if y:
                        clip(k, 2 * s + 1)
                    if s in w:
                        absolute(k, s, 1)
                    if s == 1 and norm is not None:
                        norm_apply(nc, dve, norm, norm_tiles)
                    if s == 3 and out is not None:
                        reach(dve, res_made, 2 * out + 2)
                        norm_statistics(nc, dve, out, norm_tiles)
                    if check:
                        compare_piece(k, s)
                    if project and s < 3:
                        (ky_split, q_split, k_split)[s](k.shift(1))

            split_x(0)
            weights_split(0)
            weights_split(1)
            q_split(Unit(0, 0))
            weights_split(2)
            ky_split(Unit(0, 0))
            weights_split(3)
            k_split(Unit(0, 0))
            dve.wait_ge(weights_hi, 5)
            nc.vector.tensor_tensor(wp_lo[:], wp_raw, wp_hi[:].bitcast(F32), ALU.subtract).then_inc(weights_lo, 1)
            run(slot, dve.Fori)

        @block.tensor
        def _(pe):
            misc_readers = []

            def take_misc(*readers):
                for s, count in misc_readers:
                    reach(pe, s, count)
                misc_readers[:] = readers

            def three(out, left, right, first, last):
                (lh, ll), (rh, rl) = left, right
                nc.tensor.matmul(out, lh, rh, start=first, stop=False)
                nc.tensor.matmul(out, ll, rh, start=False, stop=False)
                return nc.tensor.matmul(out, lh, rl, start=False, stop=last)

            def project_t(u, kind, done):
                reach(pe, xt_split, u.batch + 1)
                m = slice(P * u.half, P * u.half + P)
                for kt in range(DT):
                    mm = three(misc[:], (w_hi[:, kt, kind, m], w_lo[:, kt, kind, m]),
                               (xt_hi[:, kt, :], xt_lo[:, kt, :]), kt == 0, kt == DT - 1)
                mm.then_inc(done, 1)

            def q_proj(u):
                take_misc((q_lo_made, u.index + 1))
                project_t(u, 0, q_ready)

            def ky_proj(u):
                take_misc((ky_lo_made, u.index + 1))
                project_t(u, 1, ky_ready)

            def k_proj(u):
                take_misc((k_lo_made, u.index + 1))
                project_t(u, 2, k_ready)

            def v_proj(u):
                take_misc((v_staged, u.index + 1))
                m = slice(P * u.half, P * u.half + P)
                for i in range(TI):
                    tok = slice(P * i, P * i + P)
                    for kt in range(DT):
                        mm = three(misc[:, tok], (xt_hi[:, kt, tok], xt_lo[:, kt, tok]),
                                   (w_hi[:, kt, 3, m], w_lo[:, kt, 3, m]), kt == 0, kt == DT - 1)
                mm.then_inc(v_ready, 1)

            def chunk(out, left, right, u, n, c):
                r, p = rows[n % 2], n // 2
                for at, j in tiles_of(c):
                    mm = nc.tensor.matmul(out[:, at:at + T - P * j], left[u.half][r, p, P * j:P * j + P],
                                          right[u.half][r, p, P * j:T], start=True, stop=True)
                return mm

            def scores_y(k, n, c):
                if n == 0 and c == 0:
                    reach(pe, q_stacked[k.half], 16 * STACK_DMAS * (k.batch + 1))
                    reach(pe, ky_stacked[k.half], 16 * STACK_DMAS * (k.batch + 1))
                g = 3 * n + c
                reach(pe, exp_done, 24 * k.index + g - 1)
                chunk(y_bank[g % 2], ky_stack, q_stack, k, n, c).then_inc(y_scores, 1)

            def scores_w(u, n, c):
                if n == 0 and c == 0:
                    reach(pe, k_stacked[u.half], 16 * STACK_DMAS * (u.batch + 1))
                    reach(pe, qc_stacked[u.half], 16 * STACK_DMAS * (u.batch + 1))
                reach(pe, abs_done, 24 * u.index + 3 * (n - 1) + c + 1)
                chunk(w_bank[c], k_stack, qc_stack, u, n, c).then_inc(w_scores, 1)

            def scores(k, s, par, y, w):
                for c in range(CHUNKS - 1):
                    if y:
                        scores_y(k, 2 * s + par, c)
                if s == 2 and par == 0 and w:
                    sum_values(k.shift(-1))
                if w:
                    u, m = weights_of(k, s)
                    for c in range(CHUNKS):
                        scores_w(u, 2 * m + par, c)
                if y:
                    scores_y(k, 2 * s + par, CHUNKS - 1)

            def sum_keys(of, stationary, first, last):
                for turn, _ in enumerate(KEY_TILES[0]):
                    for par in range(2):
                        for g, key_tiles in enumerate(KEY_TILES):
                            j = key_tiles[turn]
                            at = SW * (2 * par + g)
                            mm = nc.tensor.matmul(acc[at:at + SW, P * j:T], stationary(j, par),
                                                  of(par)[:, W_AT[j]:W_AT[j] + T - P * j],
                                                  start=first and turn == 0, stop=last and turn == 1)
                return mm

            def sum_exps(k, s, alone):
                step = STEPS * k.index + s
                reach(pe, e_masked, 2 * (HU * k.index + 2 * s + 2))
                reach(pe, acc_copied, step)
                mm = sum_keys(lambda par: e_buf[(2 * s + par) % RING], lambda j, par: sum_exp[:], True, alone)
                if alone:
                    mm.then_inc(acc_done, 1)

            def sum_weights(k, s, alone):
                u, m = weights_of(k, s)
                step = STEPS * k.index + s
                reach(pe, w_masked, 2 * (HU * u.index + 2 * m + 2))
                reach(pe, acc_copied, step)
                reach(pe, v_spread, u.index + 1)
                sum_keys(lambda par: w_buf[(2 * m + par) % RING], lambda j, par: v_aug[u.half][:, j, 2 * m + par, :],
                         alone, True).then_inc(acc_done, 1)

            def flip_sums(step):
                reach(pe, acc_kept, step)
                reach(pe, acc_copied, step + 1)
                for i in range(TI):
                    mm = nc.tensor.transpose(flip[:, P * i:P * i + P], acc_copy[:, P * i:P * i + P], ident[:])
                mm.then_inc(acc_flipped, 1)

            def spread_c(v):
                take_misc((qc_made, v.index + 1))
                reach(pe, cols_step, 5 * (v.index + 1))
                for i in range(TI):
                    mm = nc.tensor.transpose(misc[:, P * i:P * i + P],
                                             c_spread[:, i, :, :, :].rearrange("p r d q -> p (r d q)"), ident[:])
                mm.then_inc(spread_ready, 1)

            def sum_values(v):
                take_misc((v_sum_copied, v.index + 1))
                reach(pe, v_spread, v.index + 1)
                out = misc[:].rearrange("p (i h d) -> p i h d", i=TI, h=HU)
                values = v_aug[v.half][:, :, :, 0:HD]
                mm = nc.tensor.matmul(misc[:], tri[:, 0, :], values.rearrange("p i h d -> p (i h) d"), start=True, stop=False)
                for i in range(1, TI):
                    for j in range(i):
                        mm = nc.tensor.matmul(misc[:, P * i:P * i + P], tri[:, 1, :], v_aug[v.half][:, j, :, 0:HD],
                                              start=False, stop=(i == TI - 1 and j == i - 1))
                mm.then_inc(v_sum_ready, 1)

            def turn(b, ct):
                take_misc((turned_lo, 2 * b + ct + 1))
                reach(pe, att_step, ATT_STEPS * (b + 1))
                for i in range(TI):
                    mm = nc.tensor.transpose(misc[:, P * i:P * i + P], att[:, i, P * ct:P * ct + P], ident[:])
                mm.then_inc(turned, 1)

            def project_out(b, half):
                take_misc((res_made, 2 * b + half + 1))
                reach(pe, turned_lo, 2 * (b + 1))
                for i2 in range(2):
                    i = 2 * half + i2
                    tok = slice(P * i, P * i + P)
                    for ct in range(DT):
                        mm = three(misc[:, D * i2:D * i2 + D], (att_hi[:, ct, tok], att_lo[:, ct, tok]),
                                   (wp_hi[:, ct, :], wp_lo[:, ct, :]), ct == 0, ct == DT - 1)
                mm.then_inc(proj_ready, 1)

            def slot(k, y=True, project=True, w=ALL, before=(True, True), out=None, first_in_loop=False, **_):
                if first_in_loop:
                    misc_readers[:] = [(v_staged, k.index + 1)]
                for s in range(STEPS):
                    sums = sums_of(s, y, w, before)
                    summed = (k, s - 1) if s else (k.shift(-1), STEPS - 1)
                    scores(k, s, 0, y, s in w)
                    if s == 0 and out is not None:
                        turn(out, 0)
                    if sums[0]:
                        sum_exps(*summed, not sums[1])
                    if s == 0 and out is not None:
                        turn(out, 1)
                    if s == 1 and 2 in w:
                        spread_c(k.shift(-1))
                    if s in (2, 3) and out is not None:
                        project_out(out, s - 2)
                    scores(k, s, 1, y, s in w)
                    if sums[1]:
                        sum_weights(*summed, not sums[0])
                    if project:
                        (ky_proj, q_proj, k_proj, v_proj)[s](k.shift(1))
                    if any(sums):
                        flip_sums(STEPS * k.index + s - 1)

            for n, proj in enumerate((q_proj, ky_proj, k_proj, v_proj)):
                pe.wait_ge(weights_lo, n + 1)
                proj(Unit(0, 0))
            pe.wait_ge(consts_in, 64)
            pe.wait_ge(weights_lo, 5)
            pe.wait_ge(made_once, 2)
            pe.wait_ge(acc_zeroed, 1)
            run(slot, pe.Fori)


def norm_statistics(nc, dve, b, s):
    base = LN_STEPS * b
    for i in range(TI):
        nc.vector.bn_stats(s["stats"][:, i, :], s["res"][:, i, :]).then_inc(s["ln_step"], 1)
    reach_alone(dve, s["ln_step"], base + TI, s["passed"])
    for i in range(TI):
        nc.vector.bn_aggr(s["mv"][:, i, :], s["stats"][:, i, :]).then_inc(s["ln_step"], 1)
    reach(dve, s["ln_step"], base + 2 * TI)
    nc.vector.tensor_scalar(s["var_eps"][:], s["mv"][:, :, 1], LN_EPS, None, ALU.add).then_inc(s["ln_step"], 1)


def norm_root(nc, pool, b, s):
    reach(pool, s["ln_step"], LN_STEPS * b + 2 * TI + 1)
    nc.gpsimd.tensor_tensor(s["rstd"][:], s["var_eps"][:], s["minus_half"][:], ALU.pow).then_inc(s["root_made"], 1)


def norm_apply(nc, dve, b, s):
    reach(dve, s["root_made"], b + 1)
    for i in range(TI):
        nc.vector.tensor_scalar(s["res"][:, i, :], s["res"][:, i, :], s["mv"][:, i, 0:1], s["rstd"][:, i:i + 1],
                                ALU.subtract, ALU.mult).then_inc(s["ln_step"], 1)


def feed_forward_phase(nc, a, x1, wf, differ_sum, out):
    with ExitStack() as ctx:
        def sb(name, shape, dt=F32):
            return ctx.enter_context(nc.sbuf_tensor("f_" + name, shape, dt))

        def sem(name):
            return ctx.enter_context(nc.semaphore("f_" + name))

        def bank(name):
            return ctx.enter_context(nc.psum_tensor("f_" + name, [P, 512], F32))
        RING = 4
        f_bank = [bank(f"layer_bank{i}") for i in range(RING)]
        turn_bank = [bank(f"turn_bank{i}") for i in range(DT)]
        out_bank = [bank(f"out_bank{i}") for i in range(2)]

        w_all = sb("w_all", [P, FF_TOTAL], F32R)
        w = {n: w_all[:, at:at + kt * cols].rearrange("p (k m) -> p k m", k=kt) for n, (at, kt, cols) in FF_COLS.items()}
        scales = sb("scales", [P, 4, FT])
        s3 = sb("s3", [P, 2, D])
        ident = sb("ident", [P, P])
        ones = sb("ones", [P, 2])
        inexact = sb("inexact", [1, 2], I32)
        x_turn, x_res = sb("x_turn", [P, TI, D]), sb("x_res", [P, TI, D])
        xt_hi, xt_lo = sb("xt_hi", [P, DT, T], F32R), sb("xt_lo", [P, DT, T], F32R)
        ha_hi, ha_lo = sb("ha_hi", [P, FT, T], F32R), sb("ha_lo", [P, FT, T], F32R)
        hb_hi, hb_lo = sb("hb_hi", [P, FT, T], F32R), sb("hb_lo", [P, FT, T], F32R)
        silu = [sb(f"silu{i}", [P, T]) for i in range(2)]
        h_full = [sb(f"h_full{i}", [P, T]) for i in range(2)]
        res = sb("res", [P, TI, D])
        stats, mv = sb("stats", [P, TI, 6]), sb("mv", [P, TI, 2])
        var_eps, rstd, minus_half = sb("var_eps", [P, TI]), sb("rstd", [P, TI]), sb("minus_half", [P, TI])

        ones_made = sem("ones_made")
        differ_summed, total_made, inexact_made = sem("differ_summed"), sem("total_made"), sem("inexact_made")
        ident_in, consts_in = sem("ident_in"), sem("consts_in")
        w_in = {n: sem(f"{n}_in") for n in FF_COLS}
        turn_in, res_in = sem("turn_in"), sem("res_in")
        turned = sem("turned")
        turned_hi, turned_lo = sem("turned_hi"), sem("turned_lo")
        LAYER_TILES = 4 * FT
        f_ready = sem("f_ready")
        silu_done, gate_done = sem("silu_done"), sem("gate_done")
        gelu_done = sem("gelu_done")
        h_hi_made, h_split = sem("h_hi_made"), sem("h_split")
        y_ready, y_scaled = sem("y_ready"), sem("y_scaled")
        res_made = sem("res_made")
        ln_step, root_made, minus_half_made = sem("ln_step"), sem("root_made"), sem("minus_half_made")
        stored = sem("stored")
        sp_passed, dve_passed = sem("sp_passed"), sem("dve_passed")

        norm = dict(passed=dve_passed, ln_step=ln_step, root_made=root_made, res=res, stats=stats, mv=mv, var_eps=var_eps,
                          minus_half=minus_half, rstd=rstd)
        block = ctx.enter_context(nc.Block())

        @block.sync
        def _(sp):
            sp.dma_start(x_turn[:], x1[0]).then_inc(turn_in, 16)
            sp.dma_start(ident[:], a["ident"]).then_inc(ident_in, 16)
            pieces = wf.rearrange("f s p c -> (f s) p c")
            for n, (at, kt, cols) in FF_COLS.items():
                there = w_all[:, at:at + kt * cols].rearrange("p (n c) -> p n c", c=PIECE)
                sp.dma_start(there.bitcast(F32), pieces[at // PIECE:(at + kt * cols) // PIECE].rearrange("n p c -> p n c")
                             ).then_inc(w_in[n], 16)
                if n == "w1":
                    sp.dma_start(scales[:], a["scales"]).then_inc(consts_in, 16)
                if n == "w2":
                    for i in range(2):
                        sp.dma_start(s3[:, i, :], a["s3"].partition_broadcast(P)).then_inc(consts_in, 16)

            def load(c):
                reach_alone(sp, turned, 2 * c + 2, sp_passed)
                sp.dma_start(x_turn[:], x1[(c + 1) % BATCH]).then_inc(turn_in, 16)
                reach_alone(sp, res_made, 2 * c, sp_passed)
                sp.dma_start(x_res[:], x1[c]).then_inc(res_in, 16)

            def store(c):
                reach_alone(sp, ln_step, LN_STEPS * c + LN_STEPS, sp_passed)
                sp.dma_start(out[c].rearrange("(i p) d -> p i d", p=P), res[:]).then_inc(stored, 16)

            load(0)
            with sp.Fori(1, BATCH) as c:
                load(c)
                store(c - 1)
            store(BATCH - 1)
            sp.wait_ge(stored, 16 * BATCH)

        @block.gpsimd
        def _(pool):
            nc.gpsimd.memset(minus_half[:], -0.5).then_inc(minus_half_made, 1)
            pool.wait_ge(minus_half_made, 1)
            with pool.Fori(0, BATCH) as c:
                norm_root(nc, pool, c, norm)

        @block.scalar
        def _(act):

            def turn_hi(c, ct):
                act.wait_ge(turned, 2 * c + ct + 1)
                nc.scalar.copy(xt_hi[:, ct, :], turn_bank[ct][:]).then_inc(turned_hi, 1)

            def gated(c, m):
                act.wait_ge(f_ready, LAYER_TILES * c + 2 * m + 1)
                if m >= 2:
                    act.wait_ge(gate_done, FT * c + m - 1)
                nc.scalar.activation(silu[m % 2][:], f_bank[2 * m % RING][:], ACT.Silu,
                                     scale=scales[:, 0, m:m + 1]).then_inc(silu_done, 1)

            def gate_hi(c, m):
                act.wait_ge(gate_done, FT * c + m + 1)
                nc.scalar.copy(ha_hi[:, m, :], h_full[m % 2][:]).then_inc(h_hi_made, 1)

            def gelu(c, layer, m):
                n = FT * layer + m
                act.wait_ge(f_ready, LAYER_TILES * c + FT + n + 1)
                act.wait_ge(h_split, 3 * FT * c + n - 1)
                nc.scalar.activation(h_full[m % 2][:], f_bank[m % RING][:], ACT.Gelu,
                                     scale=scales[:, 1 + layer, m:m + 1]).then_inc(gelu_done, 1)

            for ct in range(DT):
                turn_hi(0, ct)
            act.wait_ge(consts_in, 48)
            with act.Fori(0, BATCH) as c:
                for m in range(FT):
                    gated(c, m)
                    if m > 0:
                        gate_hi(c, m - 1)
                gate_hi(c, FT - 1)
                for layer in (1, 2):
                    for m in range(FT):
                        gelu(c, layer, m)
                        if layer == 2 and m in (3, 4):
                            turn_hi(c + 1, m - 3)

        @block.vector
        def _(dve):
            nc.vector.memset(ones[:], 1.0).then_inc(ones_made, 1)
            dve.wait_ge(differ_summed, 1)
            nc.vector.tensor_reduce(ones[0:1, 0:1], out_bank[0][0:1, 0:STEPS], AX.X, ALU.add).then_inc(total_made, 1)
            dve.wait_ge(total_made, 1)
            nc.vector.tensor_copy(inexact[0:1, 0:1], ones[0:1, 0:1]).then_inc(inexact_made, 1)

            def turn_lo(c, ct):
                dve.wait_ge(turned_hi, 2 * c + ct + 1)
                nc.vector.tensor_tensor(xt_lo[:, ct, :], turn_bank[ct][:], xt_hi[:, ct, :].bitcast(F32),
                                        ALU.subtract).then_inc(turned_lo, 1)

            def lo(c, n, hi_buf, lo_buf):
                m = n % FT
                dve.wait_ge(h_hi_made, 3 * FT * c + n + 1)
                nc.vector.tensor_tensor(lo_buf[:, m, :], h_full[m % 2][:], hi_buf[:, m, :].bitcast(F32),
                                        ALU.subtract).then_inc(h_split, 1)

            def gate(c, m):
                dve.wait_ge(f_ready, LAYER_TILES * c + 2 * m + 2)
                dve.wait_ge(silu_done, FT * c + m + 1)
                if m >= 2:
                    dve.wait_ge(h_split, 3 * FT * c + m - 1)
                nc.vector.scalar_tensor_tensor(out=h_full[m % 2][:], in0=f_bank[(2 * m + 1) % RING][:],
                                               scalar=scales[:, 1, m:m + 1], in1=silu[m % 2][:],
                                               op0=ALU.mult, op1=ALU.mult).then_inc(gate_done, 1)

            def output(c, part):
                if part in (1, 2):
                    half = part - 1
                    two = slice(2 * half, 2 * half + 2)
                    reach(dve, stored, 16 * c)
                    dve.wait_ge(y_ready, 2 * c + half + 1)
                    nc.vector.tensor_tensor(res[:, two, :], out_bank[half][:].rearrange("p (i d) -> p i d", i=2), s3[:],
                                            ALU.mult).then_inc(y_scaled, 1)
                if part == 3:
                    dve.wait_ge(res_in, 16 * c + 16)
                    for half in range(2):
                        two = slice(2 * half, 2 * half + 2)
                        dve.wait_ge(y_scaled, 2 * c + half + 1)
                        nc.vector.tensor_tensor(res[:, two, :], res[:, two, :], x_res[:, two, :], ALU.add).then_inc(res_made, 1)
                if part == 4:
                    dve.wait_ge(res_made, 2 * c + 2)
                    norm_statistics(nc, dve, c, norm)
                if part == 6:
                    norm_apply(nc, dve, c, norm)

            def chunk(c, before=None):
                for m in range(FT):
                    gate(c, m)
                    if m > 0:
                        lo(c, m - 1, ha_hi, ha_lo)
                    if before is not None:
                        output(before, m)
                lo(c, FT - 1, ha_hi, ha_lo)
                for layer in (1, 2):
                    hi_buf, lo_buf = ((hb_hi, hb_lo), (ha_hi, ha_lo))[layer - 1]
                    for m in range(FT):
                        dve.wait_ge(gelu_done, 2 * FT * c + FT * (layer - 1) + m + 1)
                        nc.vector.tensor_copy(hi_buf[:, m, :], h_full[m % 2][:]).then_inc(h_hi_made, 1)
                        lo(c, FT * layer + m, hi_buf, lo_buf)
                        if layer == 2 and m in (3, 4):
                            turn_lo(c + 1, m - 3)

            for ct in range(DT):
                turn_lo(0, ct)
            dve.wait_ge(consts_in, 48)
            chunk(0)
            with dve.Fori(1, BATCH) as c:
                chunk(c, c - 1)
            for part in range(FT):
                output(BATCH - 1, part)

        @block.tensor
        def _(pe):
            pe.wait_ge(ones_made, 1)
            nc.tensor.matmul(out_bank[0][0:1, 0:STEPS], ones[:, 1:2], differ_sum[:], start=True,
                             stop=True).then_inc(differ_summed, 1)
            pe.wait_ge(ident_in, 16)

            def turn(c):
                pe.wait_ge(turn_in, 16 * c + 16)
                for ct in range(DT):
                    for i in range(TI):
                        mm = nc.tensor.transpose(turn_bank[ct][:, P * i:P * i + P], x_turn[:, i, P * ct:P * ct + P], ident[:])
                    mm.then_inc(turned, 1)

            def layers(dt):
                def both(out, weight, hi, lo, first, last, weight_left=True):
                    for n, half in enumerate((hi, lo)):
                        left, right = (weight, half) if weight_left else (half, weight)
                        mm = nc.tensor.matmul(out, left.bitcast(dt), right.bitcast(dt),
                                              start=first and n == 0, stop=last and n == 1)
                    return mm

                with pe.Fori(0, BATCH) as c:
                    pe.wait_ge(turned_lo, 2 * c + 2)
                    for m in range(FT):
                        for n, name in enumerate(("w1", "w2")):
                            g = 2 * m + n
                            if m >= 2:
                                pe.wait_ge((silu_done, gate_done)[n], FT * c + m - 1)
                            if m == 0:
                                pe.wait_ge(w_in[name], 16)
                            for kt in range(DT):
                                mm = both(f_bank[g % RING][:], w[name][:, kt, P * m:P * m + P],
                                          xt_hi[:, kt, :], xt_lo[:, kt, :], kt == 0, kt == DT - 1)
                            mm.then_inc(f_ready, 1)
                    for layer, (name, hi, lo) in enumerate((("h1", ha_hi, ha_lo), ("h2", hb_hi, hb_lo))):
                        pe.wait_ge(w_in[name], 16)
                        for m in range(FT):
                            n = FT * layer + m
                            if n < RING:
                                pe.wait_ge(gate_done, FT * c + FT - 1 + n // 2)
                            else:
                                pe.wait_ge(gelu_done, 2 * FT * c + n - RING + 1)
                            for kt in range(FT):
                                if m == 0:
                                    pe.wait_ge(h_split, 3 * FT * c + FT * layer + kt + 1)
                                mm = both(f_bank[m % RING][:], w[name][:, kt, P * m:P * m + P],
                                          hi[:, kt, :], lo[:, kt, :], kt == 0, kt == FT - 1)
                            mm.then_inc(f_ready, 1)
                            if layer == 1 and m == 3:
                                pe.wait_ge(turned_lo, 2 * c + 2)
                                turn(c + 1)
                    pe.wait_ge(w_in["w3"], 16)
                    for i in range(TI):
                        tok = slice(P * i, P * i + P)
                        for kt in range(FT):
                            if i == 0:
                                pe.wait_ge(h_split, 3 * FT * c + 2 * FT + kt + 1)
                            mm = both(out_bank[i // 2][:, D * (i % 2):D * (i % 2) + D], w["w3"][:, kt, :],
                                      ha_hi[:, kt, tok], ha_lo[:, kt, tok], kt == 0, kt == FT - 1, weight_left=False)
                        if i % 2:
                            mm.then_inc(y_ready, 1)

            turn(0)
            pe.wait_ge(inexact_made, 1)
            bits = pe.value_load(inexact[0:1, 0:1], min_val=0)
            with pe.If(bits == 0):
                layers(F32R)
            with pe.Else():
                layers(F32)


def build(nc, a, out):
    x1 = nc.dram_tensor("x1", [BATCH, P, TI, D], F32, kind="Internal").ap()
    wf = nc.dram_tensor("wf_copy", [PIECES // STEPS, STEPS, P, PIECE], F32, kind="Internal").ap()
    with nc.sbuf_tensor("differ_sum", [P, STEPS], F32) as differ_sum:
        attention_phase(nc, a, x1, wf, differ_sum)
        feed_forward_phase(nc, a, x1, wf, differ_sum, out)


def kernel(L0_attn_x, L0_attn_w_qkv, L0_attn_w_ky, L0_attn_w_proj, L0_ffn_w1_w, L0_ffn_w1_s, L0_ffn_w2_w,
           L0_ffn_w2_s, L0_ffn_h1_w, L0_ffn_h1_s, L0_ffn_h2_w, L0_ffn_h2_s, L0_ffn_w3_w, L0_ffn_w3_s):
    from concourse import bacc
    from concourse.bass_utils import run_bass_kernel_spmd

    def tiles(w):
        return w.T.reshape(-1, P, w.shape[0]).transpose(1, 0, 2)

    heads = np.arange(D).reshape(2, PAIRS, 2, HD)
    order = heads.transpose(0, 2, 3, 1).reshape(-1)
    wq, wk, wv = (L0_attn_w_qkv[D * i:D * i + D] for i in range(3))
    w4 = np.stack([tiles(w) for w in (wq[order], L0_attn_w_ky[order], wk[order], wv)], axis=2)

    x = L0_attn_x
    arrays = {
        "xt": x.transpose(0, 2, 1).reshape(BATCH, DT, P, T).transpose(0, 2, 1, 3),
        "xn": x.reshape(BATCH, TI, P, D).transpose(0, 2, 1, 3),
        "w4": w4,
        "wp": tiles(L0_attn_w_proj),
        "ident": np.eye(P, dtype=np.float32),
        "tri": np.stack([np.triu(np.ones((P, P), np.float32)), np.ones((P, P), np.float32)], axis=1),
        "count": np.arange(1, T + 1, dtype=np.float32).reshape(TI, P).T,
        "wf": np.concatenate([tiles(w).reshape(P, -1) for w in
                              (L0_ffn_w1_w, L0_ffn_w2_w, L0_ffn_h1_w, L0_ffn_h2_w, L0_ffn_w3_w)], axis=1
                             ).reshape(P, PIECES, PIECE).transpose(1, 0, 2),
        "scales": np.stack([s.reshape(FT, P).T for s in
                            (L0_ffn_w1_s, L0_ffn_w2_s, L0_ffn_h1_s, L0_ffn_h2_s)], axis=1),
        "s3": L0_ffn_w3_s,
    }
    arrays = {f"in_{n}": np.ascontiguousarray(v) for n, v in arrays.items()}
    nc = bacc.Bacc("TRN2", target_bir_lowering=False, num_devices=1)
    a = {n[3:]: nc.dram_tensor(n, v.shape, mybir.dt.from_np(v.dtype), kind="ExternalInput").ap() for n, v in arrays.items()}
    out = nc.dram_tensor("out", (BATCH, T, D), F32, kind="ExternalOutput").ap()
    build(nc, a, out)
    return run_bass_kernel_spmd(nc, [arrays], core_ids=[0]).results[0]["out"]
```
